# Optimizing a Trainium2 kernel written in Bass

```python
import numpy as np
import jax
import jax.numpy as jnp

def _softmax(x, axis=-1):
    return jax.nn.softmax(x, axis=axis)

def _gelu(x):
    return jax.nn.gelu(x, approximate=True)

def _silu(x):
    return jax.nn.silu(x)

def _sigmoid(x):
    return jax.nn.sigmoid(x)

def _layernorm(x, axis=-1, eps=1e-05):
    m = jnp.mean(x, axis=axis, keepdims=True)
    v = jnp.var(x, axis=axis, keepdims=True)
    return (x - m) / jnp.sqrt(v + eps)

def _scatter_add(tgt, idx, src, axis=0):
    return tgt.at[idx].add(src)

def _segment_sum(src, seg, n):
    return jax.ops.segment_sum(src, seg, n)
kernel_name = 'mk_decoder_postln_d1_seqx_r4_0be323'

def setup_inputs(seed: int=0):
    np.random.seed(seed)
    _w = jnp.asarray

    def _rec_inputs():
        import jax
        import jax.numpy as jnp
        _rk = jax.random.key(seed)
        x = -0.0002928 + 1 * jax.random.normal(jax.random.fold_in(_rk, 1), (16, 256, 256), jnp.float32)
        _lenS = 256 - jax.random.randint(jax.random.fold_in(_rk, 7), (16,), 0, max(1, 256 // 4) + 1, jnp.int32)
        _lenS2 = 256 - jax.random.randint(jax.random.fold_in(_rk, 8), (16,), 0, max(1, 256 // 4) + 1, jnp.int32)
        _ctx_1024P = jax.random.normal(jax.random.fold_in(_rk, 11), (16, 16, 256), jnp.float32)
        _ctx_1024c = jax.random.dirichlet(jax.random.fold_in(_rk, 511), 0.3 * jnp.ones((16,), jnp.float32), (16, 256))
        _ctx_1024t = jnp.einsum('bsk,bkd->bsd', _ctx_1024c, _ctx_1024P)
        _ctx_1024t = _ctx_1024t * jax.lax.rsqrt(jnp.mean(jnp.square(_ctx_1024t)) + 1e-12) * 0.953939
        ctx_1024 = -1.39393e-06 + 0.999914 * (_ctx_1024t + 0.3 * jax.random.normal(jax.random.fold_in(_rk, 611), (16, 256, 256), jnp.float32))
        return (x, ctx_1024)
    x, ctx_1024 = _rec_inputs()

    def _L0_attn_setup():
        import jax, jax.numpy as jnp
        import numpy as np
        STATE_DIM = 256
        INPUT_DIM = 256
        OUTPUT_DIM = 256
        BATCH = 8
        SEQ = 512
        key = jax.random.key(seed)
        k_x, k_a, k_b, k_w, k_bias = jax.random.split(key, 5)
        x = jax.random.normal(k_x, (BATCH, SEQ, INPUT_DIM), dtype=jnp.float32)
        A = jax.random.uniform(k_a, (STATE_DIM,), dtype=jnp.float32, minval=0.0, maxval=0.99)
        B = jax.random.normal(k_b, (STATE_DIM, INPUT_DIM), dtype=jnp.float32) / np.sqrt(INPUT_DIM)
        W = jax.random.normal(k_w, (OUTPUT_DIM, STATE_DIM), dtype=jnp.float32) / np.sqrt(STATE_DIM)
        b = jax.random.normal(k_bias, (OUTPUT_DIM,), dtype=jnp.float32) * 0.01
        return {'x': x, 'A': A, 'B': B, 'W': W, 'b': b}
    _L0_attn_all = _L0_attn_setup()
    _L0_attn_in = {k: v for k, v in _L0_attn_all.items() if k in ('A', 'B', 'W', 'b')}
    del _L0_attn_all

    def _L0_xattn_setup():
        import jax, jax.numpy as jnp
        import numpy as np
        H = 16
        D_MODEL = 256
        D_K = D_MODEL // H
        WINDOW = 50
        ROPE_BASE = 10000.0

        def _rope_tables(seq_len, dim, dtype):
            inv_freq = 1.0 / ROPE_BASE ** (jnp.arange(0, dim, 2, dtype=jnp.float32) / dim)
            t = jnp.arange(seq_len, dtype=jnp.float32)
            freqs = t[:, None] * inv_freq[None, :]
            emb = jnp.concatenate([freqs, freqs], axis=-1)
            return (jnp.cos(emb).astype(dtype), jnp.sin(emb).astype(dtype))

        def _rotate_half(x):
            d = x.shape[-1] // 2
            return jnp.concatenate([-x[..., d:], x[..., :d]], axis=-1)
        key = jax.random.key(seed)
        ks = jax.random.split(key, 11)
        B, S = (2, 512)
        scale = 1.0 / np.sqrt(D_MODEL)
        inp = {'query': jax.random.normal(ks[0], (B, S, D_MODEL), jnp.float32), 'key': jax.random.normal(ks[1], (B, S, D_MODEL), jnp.float32), 'value': jax.random.normal(ks[2], (B, S, D_MODEL), jnp.float32), 'Wq': jax.random.normal(ks[3], (D_MODEL, D_MODEL), jnp.float32) * scale, 'bq': jnp.zeros((D_MODEL,), jnp.float32), 'Wk': jax.random.normal(ks[4], (D_MODEL, D_MODEL), jnp.float32) * scale, 'bk': jnp.zeros((D_MODEL,), jnp.float32), 'Wv': jax.random.normal(ks[5], (D_MODEL, D_MODEL), jnp.float32) * scale, 'bv': jnp.zeros((D_MODEL,), jnp.float32), 'Wo': jax.random.normal(ks[6], (D_MODEL, D_MODEL), jnp.float32) * scale, 'bo': jnp.zeros((D_MODEL,), jnp.float32)}
        return inp
    _L0_xattn_all = _L0_xattn_setup()
    _L0_xattn_in = {k: v for k, v in _L0_xattn_all.items() if k in ('Wq', 'bq', 'Wk', 'bk', 'Wv', 'bv', 'Wo', 'bo')}
    del _L0_xattn_all

    def _L0_ffn_setup():
        import jax, jax.numpy as jnp
        import numpy as np
        import math
        B, S, D = (4, 512, 256)
        E, DFF = (16, 512)
        CAP_FACTOR = 2.0
        ROUTER_HIDDEN = 128
        CAPACITY = int(math.ceil(S * CAP_FACTOR / E))
        key = jax.random.key(seed)
        ks = jax.random.split(key, 6)

        def uinit(k, shape, fan_in):
            bound = math.sqrt(3.0) * math.sqrt(1.0 / 3.0) / math.sqrt(fan_in)
            return jax.random.uniform(k, shape, jnp.float32, -bound, bound)
        return {'hidden_states': jax.random.normal(ks[0], (B, S, D), jnp.float32), 'router_w1': jax.random.normal(ks[1], (D, ROUTER_HIDDEN), jnp.float32) / math.sqrt(D), 'router_w2': jax.random.normal(ks[2], (ROUTER_HIDDEN, E), jnp.float32) / math.sqrt(ROUTER_HIDDEN), 'w1': uinit(ks[3], (E, D, DFF), D), 'w2': uinit(ks[4], (E, D, DFF), D), 'w3': uinit(ks[5], (E, DFF, D), DFF)}
    _L0_ffn_all = _L0_ffn_setup()
    _L0_ffn_in = {k: v for k, v in _L0_ffn_all.items() if k in ('router_w1', 'router_w2', 'w1', 'w2', 'w3')}
    del _L0_ffn_all
    return {'x': x, 'ctx_1024': ctx_1024, 'L0_attn_A': _L0_attn_in['A'], 'L0_attn_B': _L0_attn_in['B'], 'L0_attn_W': _L0_attn_in['W'], 'L0_attn_b': _L0_attn_in['b'], 'L0_xattn_Wq': _L0_xattn_in['Wq'], 'L0_xattn_bq': _L0_xattn_in['bq'], 'L0_xattn_Wk': _L0_xattn_in['Wk'], 'L0_xattn_bk': _L0_xattn_in['bk'], 'L0_xattn_Wv': _L0_xattn_in['Wv'], 'L0_xattn_bv': _L0_xattn_in['bv'], 'L0_xattn_Wo': _L0_xattn_in['Wo'], 'L0_xattn_bo': _L0_xattn_in['bo'], 'L0_ffn_router_w1': _L0_ffn_in['router_w1'], 'L0_ffn_router_w2': _L0_ffn_in['router_w2'], 'L0_ffn_w1': _L0_ffn_in['w1'], 'L0_ffn_w2': _L0_ffn_in['w2'], 'L0_ffn_w3': _L0_ffn_in['w3']}

def reference(x, ctx_1024, L0_attn_A, L0_attn_B, L0_attn_W, L0_attn_b, L0_xattn_Wq, L0_xattn_bq, L0_xattn_Wk, L0_xattn_bk, L0_xattn_Wv, L0_xattn_bv, L0_xattn_Wo, L0_xattn_bo, L0_ffn_router_w1, L0_ffn_router_w2, L0_ffn_w1, L0_ffn_w2, L0_ffn_w3):
    import jax
    import jax.numpy as jnp

    def _L0_attn_ref(x, A, B, W, b):
        import jax, jax.numpy as jnp
        import numpy as np
        STATE_DIM = 256
        INPUT_DIM = 256
        OUTPUT_DIM = 256
        BATCH = 8
        SEQ = 512
        u = jnp.einsum('bld,nd->bln', x, B)
        aa = jnp.broadcast_to(A, u.shape)

        def combine(c1, c2):
            a1, b1 = c1
            a2, b2 = c2
            return (a1 * a2, a2 * b1 + b2)
        _, h = jax.lax.associative_scan(combine, (aa, u), axis=1)
        return jnp.einsum('bln,on->blo', h, W) + b

    def _L0_xattn_ref(query, key, value, Wq, bq, Wk, bk, Wv, bv, Wo, bo):
        import jax, jax.numpy as jnp
        import numpy as np
        H = 16
        D_MODEL = 256
        D_K = D_MODEL // H
        WINDOW = 50
        ROPE_BASE = 10000.0

        def _rope_tables(seq_len, dim, dtype):
            inv_freq = 1.0 / ROPE_BASE ** (jnp.arange(0, dim, 2, dtype=jnp.float32) / dim)
            t = jnp.arange(seq_len, dtype=jnp.float32)
            freqs = t[:, None] * inv_freq[None, :]
            emb = jnp.concatenate([freqs, freqs], axis=-1)
            return (jnp.cos(emb).astype(dtype), jnp.sin(emb).astype(dtype))

        def _rotate_half(x):
            d = x.shape[-1] // 2
            return jnp.concatenate([-x[..., d:], x[..., :d]], axis=-1)
        B, S, _ = query.shape

        def proj(x, W, b):
            return (x @ W.T + b).reshape(B, S, H, D_K).transpose(0, 2, 1, 3)
        q = proj(query, Wq, bq)
        k = proj(key, Wk, bk)
        v = proj(value, Wv, bv)
        cos, sin = _rope_tables(S, D_K, q.dtype)
        q = q * cos + _rotate_half(q) * sin
        k = k * cos + _rotate_half(k) * sin
        scores = jnp.einsum('bhqd,bhkd->bhqk', q, k) / np.sqrt(D_K)
        idx = jnp.arange(S)
        dist = jnp.abs(idx[None, :] - idx[:, None])
        scores = jnp.where(dist <= WINDOW, scores, jnp.asarray(-1000000000.0, scores.dtype))
        p = jax.nn.softmax(scores, axis=-1)
        out = jnp.einsum('bhqk,bhkd->bhqd', p, v)
        out = out.transpose(0, 2, 1, 3).reshape(B, S, D_MODEL)
        return out @ Wo.T + bo

    def _L0_ffn_ref(hidden_states, router_w1, router_w2, w1, w2, w3):
        import jax, jax.numpy as jnp
        import numpy as np
        import math
        B, S, D = (4, 512, 256)
        E, DFF = (16, 512)
        CAP_FACTOR = 2.0
        ROUTER_HIDDEN = 128
        CAPACITY = int(math.ceil(S * CAP_FACTOR / E))
        b, s, d = hidden_states.shape
        e = w1.shape[0]
        cap = CAPACITY
        router_logits = jax.nn.silu(hidden_states @ router_w1) @ router_w2
        expert_probs = jax.nn.softmax(router_logits.transpose(0, 2, 1), axis=-1)
        expert_weights, token_indices = jax.lax.top_k(expert_probs, cap)
        expert_weights = expert_weights / (expert_weights.sum(-1, keepdims=True) + 1e-09)
        expert_inputs = jax.vmap(lambda h, i: h[i])(hidden_states, token_indices)
        gate = jax.nn.silu(jnp.einsum('becd,edf->becf', expert_inputs, w1))
        value = jnp.einsum('becd,edf->becf', expert_inputs, w2)
        expert_out = jnp.einsum('becf,efd->becd', gate * value, w3)
        weighted = expert_out * expert_weights[..., None]

        def combine(idx, vals):
            return jnp.zeros((s, d), vals.dtype).at[idx.reshape(-1)].add(vals.reshape(-1, d))
        output = jax.vmap(combine)(token_indices, weighted)
        return output
    x = _layernorm(x + _L0_attn_ref(x, L0_attn_A, L0_attn_B, L0_attn_W, L0_attn_b), axis=-1)
    x = _layernorm(x + _L0_xattn_ref(x, ctx_1024, ctx_1024, L0_xattn_Wq, L0_xattn_bq, L0_xattn_Wk, L0_xattn_bk, L0_xattn_Wv, L0_xattn_bv, L0_xattn_Wo, L0_xattn_bo), axis=-1)
    x = _layernorm(x + _L0_ffn_ref(x, L0_ffn_router_w1, L0_ffn_router_w2, L0_ffn_w1, L0_ffn_w2, L0_ffn_w3), axis=-1)
    return x

_drawn_inputs = setup_inputs


def setup_inputs(seed=0):
    import zlib

    import numpy as np

    out = dict(_drawn_inputs(seed))
    spreads = {'L0_xattn_bq': (0.0, 0.403),
     'L0_xattn_bk': (0.0, 0.8),
     'L0_xattn_bv': (0.0, 0.1),
     'L0_xattn_bo': (0.0, 0.1)}
    factors = {'L0_attn_b': 8.0,
     'L0_ffn_router_w1': 8.0,
     'L0_ffn_router_w2': 8.0,
     'L0_ffn_w1': 8.0,
     'L0_ffn_w2': 8.0,
     'L0_ffn_w3': 8.0}
    for name, (base, spread) in spreads.items():
        noise = np.random.default_rng([zlib.crc32(name.encode()), seed]).standard_normal(out[name].shape)
        drawn = base * np.exp(spread * noise) if base else spread * noise
        out[name] = jnp.asarray(drawn.astype(out[name].dtype))
    for name, factor in factors.items():
        out[name] = (out[name] * factor).astype(out[name].dtype)
    return out
```

```python
from contextlib import ExitStack

import concourse.bass as bass
from concourse import mybir

F32 = mybir.dt.float32
U32 = mybir.dt.uint32
ALU = mybir.AluOpType
ACT = mybir.ActivationFunctionType
AX = mybir.AxisListType

P = 128
NB = 16
S = 256
D = 256
KT = D // P
TT = S // P
NH = 16
DH = D // NH
HG = 4
NG = NH // HG
HPT = P // DH
WINDOW = 50
HID = 128
NE = 16
CAP = 64
FF = 512
FT = FF // P
PAIRS = NE // 2
EPS = 1e-5
MASKED = -4e9
BIG = 3e38


class Iter:

    def __init__(self, j, r):
        self.j, self.r = j, r
        self.fixed = isinstance(j, int)
        self.i = 2 * j + r

    def lin(self, a, c):
        return self.j * (2 * a) + (a * self.r + c)

    def half(self, a, c):
        return self.j * a + (a * self.r + c) // 2

    def loads(self, d):
        return self.j * 48 + 48 * ((self.r + d) // 2 + 1)

    def batch(self, d):
        return not self.fixed or 0 <= self.i + d < NB

    def at_least(self, n):
        return not self.fixed or self.i >= n


FULL = ["U", "K", "V", "O", "Y", "X", "Q", "OX", "R"]
FRONT = [n for n in FULL if n not in ("O", "OX", "R")]
OUTS = ["O", "OX", "R"]
NF, NFR, NO = len(FULL), len(FRONT), len(OUTS)


class Use:

    def __init__(self, it, name):
        if it.fixed and it.i == -1:
            n = FRONT.index(name)
        elif it.fixed and it.i == 0:
            n = NFR + FRONT.index(name)
        elif it.fixed and it.i >= NB - 1:
            n = 2 * NFR + NF * (NB - 2) + NO * (it.i - NB + 1) + OUTS.index(name)
        else:
            c = 2 * NFR - NF + FULL.index(name)
            self.bank = (NF * it.r + c) % 2
            self.ready = it.lin(NF, c + 1)
            self.before = it.half(NF, c)
            self.first = False
            return
        self.bank, self.ready, self.before, self.first = n % 2, n + 1, n // 2, n < 2


def estimate_deviation(act, var, log, guess, chain, before, ready):
    act.activation(log, var, ACT.Ln, bias=EPS).then_inc(chain, 1)
    act.wait_ge(chain, before + 1)
    act.activation(guess, log, ACT.Exp, scale=-0.5).then_inc(ready, 1)


def refine_deviation(pool, met, var, guess, tmp, rstd, chain, before, ready):
    met()
    pool.tensor_scalar(rstd, var, EPS, None, ALU.add)
    pool.tensor_tensor(tmp, guess, guess, ALU.mult).then_inc(chain, 1)
    pool.wait_ge(chain, before + 1)
    pool.tensor_tensor(tmp, tmp, rstd, ALU.mult).then_inc(chain, 1)
    pool.wait_ge(chain, before + 2)
    met()
    pool.tensor_scalar(tmp, tmp, -0.5, 1.5, ALU.mult, ALU.add).then_inc(chain, 1)
    pool.wait_ge(chain, before + 3)
    pool.tensor_tensor(rstd, guess, tmp, ALU.mult).then_inc(ready, 1)


def ln_before(it, name):
    if it.fixed and it.i < 1:
        return it.i + 1
    if it.fixed and it.i >= NB:
        return 2 * NB - 1
    return it.lin(2, 0 if name == "O" else 1)


def mixing(nc, dram, keep):
    with ExitStack() as ctx:
        def sb(name, *shape):
            return ctx.enter_context(nc.sbuf_tensor(name, [P, *shape], F32))

        def ps(name):
            return ctx.enter_context(nc.psum_tensor(name, [P, 512], F32))

        def sem(name):
            return ctx.enter_context(nc.semaphore(name))

        x2, r1 = keep["x2"], keep["r1"]
        ident = keep["ident"]
        wb, ww = sb("wb", KT, D), sb("ww", KT, D)
        wq, wk, wv = sb("wq", KT, D), sb("wk", KT, D), sb("wv", KT, D)
        wo = sb("wo", NG, D)
        rw1 = sb("rw1", KT, HID)
        cos, sin = sb("cos", S), sb("sin", S)
        band = sb("band", TT, S)
        head_rows = sb("head_rows", HPT)
        acol, bq, bk = sb("acol", KT), sb("bq", KT), sb("bk", KT)
        b_mix, bv = sb("b_mix", D), sb("bv", D)
        xT = [sb(f"xT{n}", KT, S) for n in range(2)]
        cT = [sb(f"cT{n}", KT, S) for n in range(2)]
        xin = [sb(f"xin{n}", TT, D) for n in range(2)]
        state = sb("state", KT, S)
        xb = sb("xb", TT, D)
        pre = sb("pre", TT, D)
        stats, mv, rstd = sb("stats", TT, 6), sb("mv", TT, 2), sb("rstd", TT)
        log, guess, newton = sb("log", TT), sb("guess", TT), sb("newton", TT)
        x1 = [sb(f"x1_{n}", TT, D) for n in range(2)]
        x1T = sb("x1T", KT, S)
        raw_q, raw_k = sb("raw_q", KT, S), sb("raw_k", KT, S)
        rot = sb("rot", KT, S)
        rope = sb("rope", KT, S)
        kr = [sb(f"kr{n}", KT, S) for n in range(2)]
        qm = [sb(f"qm{n}", NH, S) for n in range(2)]
        vp = [sb(f"vp{n}", TT, NH, 2 * DH) for n in range(2)]
        scored = [sb(f"scored{n}", TT, S) for n in range(2)]
        nmax = [sb(f"nmax{n}", TT) for n in range(2)]
        probs = [sb(f"probs{n}", TT, S) for n in range(2)]
        NPT = 8
        probsT = [sb(f"probsT{n}", TT, S) for n in range(NPT)]
        sums = sb("sums", S)
        attnT = [sb(f"attnT{n}", NG, S) for n in range(2)]
        x2cur = sb("x2cur", TT, D)
        x2T = sb("x2T", KT, S)

        work = [ps(f"work{n}") for n in range(2)]
        score = [ps(f"score{n}") for n in range(2)]
        turned = [ps(f"turned{n}") for n in range(2)]
        attn = [ps(f"attn{n}") for n in range(2)]

        dve_met, pool_met = sem("dve_met"), sem("pool_met")
        const_in = sem("const_in")
        batch_in = [sem(f"batch_in{n}") for n in range(2)]
        ones_set = sem("ones_set")
        work_ready = sem("work_ready")
        work_free = [sem(f"work_free{n}") for n in range(2)]
        xb_ready = sem("xb_ready")
        state_ready = sem("state_ready")
        log_chain, guess_ready, newton_chain, rstd_ready = sem("log_chain"), sem("guess_ready"), sem("newton_chain"), sem("rstd_ready")
        ln_chain, norm_chain, rope_chain = sem("ln_chain"), sem("norm_chain"), sem("rope_chain")
        x1_ready, x1T_ready = sem("x1_ready"), sem("x1T_ready")
        raw_ready, rot_chain, rot_ready = sem("raw_ready"), sem("rot_chain"), sem("rot_ready")
        kr_ready, qr_ready, qm_ready = sem("kr_ready"), sem("qr_ready"), sem("qm_ready")
        vp_ready = sem("vp_ready")
        score_ready, scored_ready = sem("score_ready"), sem("scored_ready")
        probs_ready, turned_ready = sem("probs_ready"), sem("turned_ready")
        probsT_even, probsT_odd = sem("probsT_even"), sem("probsT_odd")
        attn_ready, attnT_ready = sem("attn_ready"), sem("attnT_ready")
        x2_ready, x2_kept, x2T_ready = sem("x2_ready"), sem("x2_kept"), sem("x2T_ready")

        consts = [
            (wb, dram["mix_BT"].rearrange("(k p) n -> p k n", p=P)),
            (ww, dram["mix_WT"].rearrange("(k p) n -> p k n", p=P)),
            (wq, dram["WqT"].rearrange("(k p) n -> p k n", p=P)),
            (wk, dram["WkT"].rearrange("(k p) n -> p k n", p=P)),
            (wv, dram["WvT"].rearrange("(k p) n -> p k n", p=P)),
            (rw1, dram["rw1"].rearrange("(k p) n -> p k n", p=P)),
            (cos, dram["cos"]), (sin, dram["sin"]),
            (band, dram["band"].rearrange("(t p) k -> p t k", p=P)),
            (head_rows, dram["head_rows"]), (ident, dram["ident"]),
            (acol, dram["mix_A"]),
            (bq, dram["bq"]),
            (bk, dram["bk"]),
            (b_mix, dram["mix_b"].partition_broadcast(P)),
            (bv, dram["bv"].partition_broadcast(P)),
        ]
        wo_rows = dram["WoT"].rearrange("(g q d) n -> q d g n", g=NG, q=HG)
        CONST_DMAS = len(consts) + HG + 1

        block = ctx.enter_context(nc.Block())

        @block.sync
        def _(sp):
            def load(par, b):
                sp.dma_start(xT[par][:], dram["xT"][b].rearrange("(k p) s -> p k s", p=P)).then_inc(batch_in[par], 16)
                sp.dma_start(cT[par][:], dram["cT"][b].rearrange("(k p) s -> p k s", p=P)).then_inc(batch_in[par], 16)
                sp.dma_start(xin[par][:], dram["x"][b].rearrange("(t p) d -> p t d", p=P)).then_inc(batch_in[par], 16)

            load(0, 0)
            for tile, src in consts:
                sp.dma_start(tile[:], src).then_inc(const_in, 16)
            sp.wait_ge(ones_set, 3)
            for q in range(HG):
                sp.dma_start(wo[32 * q:32 * q + DH, :, :], wo_rows[q]).then_inc(const_in, 16)
            sp.dma_start(wo[DH:DH + 1, 0, :], dram["bo"].partition_broadcast(1)).then_inc(const_in, 16)
            load(1, 1)
            for b in (2, 3):
                sp.wait_ge(work_ready, Use(Iter(0, b - 3), "V").ready)
                sp.wait_ge(xb_ready, b - 1)
                load(b % 2, b)
            with sp.Fori(0, (NB - 4) // 2) as j:
                for r in range(2):
                    b = j * 2 + (4 + r)
                    sp.wait_ge(work_ready, Use(Iter(j, r + 1), "V").ready)
                    sp.wait_ge(xb_ready, b - 1)
                    load(r, b)

        @block.gpsimd
        def _(pool):
            nc.gpsimd.memset(wo[:], 0.0).then_inc(ones_set, 1)
            for n in range(2):
                nc.gpsimd.memset(vp[n][:], 1.0).then_inc(ones_set, 1)
            pool.wait_ge(const_in, 16 * CONST_DMAS)

            def rotate(it, raw, out, done, which):
                pool.wait_ge(raw_ready, it.lin(2, 3 + which))
                pool_mul = nc.gpsimd.tensor_tensor(rope[:], raw[:], cos[:].unsqueeze(1).to_broadcast([P, KT, S]), ALU.mult)
                pool_mul.then_inc(rope_chain, 1)
                pool.wait_ge(rope_chain, it.lin(2, 3 + which))
                pool.wait_ge(rot_ready, it.lin(2, 3 + which))
                nc.gpsimd.tensor_tensor(out[:], rope[:], rot[:], ALU.add).then_inc(done, 1)

            def met():
                pool.sem_inc(pool_met, 1)

            def inverse_deviation(n):
                pool.wait_ge(guess_ready, n + 1)
                refine_deviation(pool, met, mv[:, :, 1], guess[:], newton[:], rstd[:], newton_chain, n * 3, rstd_ready)

            def step(it):
                par = (it.r + 1) % 2
                front, outs = it.batch(1), it.batch(-1)
                if front:
                    pool.wait_ge(batch_in[par], it.loads(1))
                    if it.at_least(0):
                        pool.wait_ge(x1_ready, it.lin(1, 1))
                    nc.gpsimd.tensor_tensor(xb[:], xin[par][:], b_mix[:].unsqueeze(1).to_broadcast([P, TT, D]),
                                            ALU.add).then_inc(xb_ready, 1)
                    if it.at_least(1):
                        pool.wait_ge(score_ready, it.lin(NH, 0))
                    rotate(it, raw_k, kr[par], kr_ready, 0)
                if outs:
                    inverse_deviation(ln_before(it, "O"))
                    pool.wait_ge(x2_ready, it.lin(1, 0))
                    nc.gpsimd.tensor_copy(x2[:, bass.ds(it.lin(TT * D, -TT * D), TT * D)],
                                          x2cur[:].rearrange("p t d -> p (t d)")).then_inc(x2_kept, 1)
                if front:
                    inverse_deviation(ln_before(it, "Y"))
                    rotate(it, raw_q, raw_q, qr_ready, 1)
                    pool.wait_ge(qr_ready, it.lin(1, 2))
                    met()
                    for h in range(NH):
                        nc.gpsimd.tensor_scalar(qm[par][:, h, :], raw_q[:, h // HPT, :],
                                                head_rows[:, h % HPT:h % HPT + 1], None,
                                                ALU.mult).then_inc(qm_ready, 1)

            for i in (-1, 0):
                step(Iter(0, i))
            with pool.Fori(0, (NB - 2) // 2) as j:
                for r in (1, 2):
                    step(Iter(j, r))
            for i in (NB - 1, NB):
                step(Iter(0, i))

        @block.tensor
        def _(pe):
            pe.wait_ge(const_in, 16 * CONST_DMAS)

            def begin(u):
                if not u.first:
                    pe.wait_ge(work_free[u.bank], u.before)
                return work[u.bank]

            def heads(it, t):
                if it.batch(0):
                    if not (it.fixed and it.i == 0 and t < 2):
                        pe.wait_ge(scored_ready, it.lin(NH, t - 1))
                    if t == 0:
                        pe.wait_ge(kr_ready, it.lin(1, 1))
                    pe.wait_ge(qm_ready, it.lin(NH, t + 1))
                    for q in range(TT):
                        mm = nc.tensor.matmul(score[t % 2][:, q * S:(q + 1) * S],
                                              qm[it.r % 2][:, t, q * P:(q + 1) * P],
                                              kr[it.r % 2][:, t // HPT, :], start=True, stop=True)
                    mm.then_inc(score_ready, 1)
                if it.batch(0) if t >= 2 else it.batch(-1):
                    pe.wait_ge(probs_ready, it.lin(NH, t - 1))
                    if not (it.fixed and it.i == 0 and t < 4):
                        pe.wait_ge(probsT_odd if t % 2 else probsT_even, it.half(NH, t - 2))
                    for q in range(TT):
                        for k in range(TT):
                            mm = nc.tensor.transpose(turned[t % 2][:, k * S + q * P:k * S + (q + 1) * P],
                                                     probs[t % 2][:, q, k * P:(k + 1) * P], ident[:])
                    mm.then_inc(turned_ready, 1)
                if t % 4 == 3 and (it.batch(0) if t >= 7 else it.batch(-1)):
                    g = (t - 7) // 4
                    vpar = (it.r if g >= 0 else it.r + 1) % 2
                    pe.wait_ge(probsT_even, it.lin(2 * NG, 2 * (g + 1)))
                    pe.wait_ge(probsT_odd, it.lin(2 * NG, 2 * (g + 1)))
                    pe.wait_ge(vp_ready, it.lin(1, 1 if g >= 0 else 0))
                    if not (it.fixed and it.i == 0 and g < 2):
                        pe.wait_ge(attnT_ready, it.lin(NG, g - 1))
                    for k in range(TT):
                        for q in range(HG):
                            h = HG * (g % NG) + q
                            mm = nc.tensor.matmul(attn[g % 2][32 * q:32 * q + 32, 0:S], vp[vpar][:, k, h, :],
                                                  probsT[(HG * g + q) % NPT][:, k, :],
                                                  start=(k == 0), stop=(k == TT - 1))
                    mm.then_inc(attn_ready, 1)

            def step(it):
                par = (it.r + 1) % 2
                front, outs = it.batch(1), it.batch(-1)
                for t in range(NH):
                    heads(it, t)
                    if front and t == 0:
                        u = Use(it, "U")
                        pe.wait_ge(batch_in[par], it.loads(1))
                        w = begin(u)
                        for n in range(KT):
                            for k in range(KT):
                                mm = nc.tensor.matmul(w[:, n * S:(n + 1) * S], wb[:, k, n * P:(n + 1) * P],
                                                      xT[par][:, k, :], start=(k == 0), stop=(k == KT - 1))
                        mm.then_inc(work_ready, 1)
                    if front and t == 1:
                        w = begin(Use(it, "K"))
                        for n in range(KT):
                            for k in range(KT):
                                mm = nc.tensor.matmul(w[:, n * S:(n + 1) * S], wk[:, k, n * P:(n + 1) * P],
                                                      cT[par][:, k, :], start=(k == 0), stop=(k == KT - 1))
                        mm.then_inc(work_ready, 1)
                    if front and t == 2:
                        w = begin(Use(it, "V"))
                        for n in range(TT):
                            for k in range(KT):
                                mm = nc.tensor.matmul(w[:, n * D:(n + 1) * D], cT[par][:, k, n * P:(n + 1) * P],
                                                      wv[:, k, :], start=(k == 0), stop=(k == KT - 1))
                        mm.then_inc(work_ready, 1)
                    if outs and t == 5:
                        w = begin(Use(it, "O"))
                        pe.wait_ge(attnT_ready, it.lin(NG, 0))
                        for n in range(TT):
                            for g in range(NG):
                                mm = nc.tensor.matmul(w[:, n * D:(n + 1) * D], attnT[(it.r + 1) % 2][:, g, n * P:(n + 1) * P],
                                                      wo[:, g, :], start=(g == 0), stop=(g == NG - 1))
                        mm.then_inc(work_ready, 1)
                    if front and t == 6:
                        w = begin(Use(it, "Y"))
                        pe.wait_ge(state_ready, it.lin(1, 2))
                        for n in range(TT):
                            for k in range(KT):
                                mm = nc.tensor.matmul(w[:, n * D:(n + 1) * D], state[:, k, n * P:(n + 1) * P],
                                                      ww[:, k, :], start=(k == 0), stop=(k == KT - 1))
                        mm.then_inc(work_ready, 1)
                    if front and t == 8:
                        w = begin(Use(it, "X"))
                        pe.wait_ge(x1_ready, it.lin(1, 2))
                        for k in range(KT):
                            for n in range(TT):
                                mm = nc.tensor.transpose(w[:, k * S + n * P:k * S + (n + 1) * P],
                                                         x1[par][:, n, k * P:(k + 1) * P], ident[:])
                        mm.then_inc(work_ready, 1)
                    if front and t == 9:
                        w = begin(Use(it, "Q"))
                        pe.wait_ge(x1T_ready, it.lin(1, 2))
                        for n in range(KT):
                            for k in range(KT):
                                mm = nc.tensor.matmul(w[:, n * S:(n + 1) * S], wq[:, k, n * P:(n + 1) * P],
                                                      x1T[:, k, :], start=(k == 0), stop=(k == KT - 1))
                        mm.then_inc(work_ready, 1)
                    if outs and t == 11:
                        w = begin(Use(it, "OX"))
                        pe.wait_ge(x2_ready, it.lin(1, 0))
                        for k in range(KT):
                            for n in range(TT):
                                mm = nc.tensor.transpose(w[:, k * S + n * P:k * S + (n + 1) * P],
                                                         x2cur[:, n, k * P:(k + 1) * P], ident[:])
                        mm.then_inc(work_ready, 1)
                    if outs and t == 13:
                        w = begin(Use(it, "R"))
                        pe.wait_ge(x2T_ready, it.lin(1, 0))
                        for k in range(KT):
                            mm = nc.tensor.matmul(w[:, 0:S], rw1[:, k, :], x2T[:, k, :],
                                                  start=(k == 0), stop=(k == KT - 1))
                        mm.then_inc(work_ready, 1)

            for i in (-1, 0):
                step(Iter(0, i))
            with pe.Fori(0, (NB - 2) // 2) as j:
                for r in (1, 2):
                    step(Iter(j, r))
            for i in (NB - 1, NB):
                step(Iter(0, i))

        @block.scalar
        def _(act):
            act.wait_ge(const_in, 16 * CONST_DMAS)
            act.preload_act_table(ACT.Ln)

            def step(it):
                front, outs = it.batch(1), it.batch(-1)
                for t in range(NH):
                    if it.batch(0):
                        act.wait_ge(scored_ready, it.lin(NH, t + 1))
                        if not (it.fixed and it.i == 0 and t < 2):
                            act.wait_ge(turned_ready, it.lin(NH, t - 1))
                        for q in range(TT):
                            a = nc.scalar.activation(probs[t % 2][:, q, :], scored[t % 2][:, q, :], ACT.Exp,
                                                     bias=nmax[t % 2][:, q:q + 1], scale=-1.0)
                        a.then_inc(probs_ready, 1)
                    if t % 2 == 0 and (it.batch(0) if t >= 3 else it.batch(-1)):
                        act.wait_ge(turned_ready, it.lin(NH, t - 2))
                        if not (it.fixed and it.i == 0 and t - 3 < NPT):
                            act.wait_ge(attn_ready, it.lin(NG, (t - 3) // HG - 1))
                        nc.scalar.copy(probsT[(t - 3) % NPT][:].rearrange("p t s -> p (t s)"),
                                       turned[1][:]).then_inc(probsT_odd, 1)
                    for when, name, raw, bias, which in ((2, "K", raw_k, bk, 0), (10, "Q", raw_q, bq, 1)):
                        if front and t == when:
                            u = Use(it, name)
                            act.wait_ge(work_ready, u.ready)
                            if it.at_least(0):
                                if which:
                                    act.wait_ge(qm_ready, it.lin(NH, NH))
                                else:
                                    act.wait_ge(kr_ready, it.lin(1, 1))
                            for k in range(KT):
                                a = nc.scalar.activation(raw[:, k, :], work[u.bank][:, k * S:(k + 1) * S],
                                                         ACT.Identity, bias=bias[:, k:k + 1])
                            a.then_inc(work_free[u.bank], 1)
                            act.wait_ge(work_free[u.bank], u.before + 1)
                            act.sem_inc(raw_ready, 1)
                    for when, name, there in ((6, "O", outs), (7, "Y", front)):
                        if there and t == when:
                            n = ln_before(it, name)
                            act.wait_ge(ln_chain, n * 2 + 2)
                            estimate_deviation(act, mv[:, :, 1], log[:], guess[:], log_chain, n, guess_ready)
                    if front and t == 9:
                        u = Use(it, "X")
                        act.wait_ge(work_ready, u.ready)
                        nc.scalar.copy(x1T[:].rearrange("p k s -> p (k s)"), work[u.bank][:]).then_inc(work_free[u.bank], 1)
                        act.wait_ge(work_free[u.bank], u.before + 1)
                        act.sem_inc(x1T_ready, 1)
                    if outs and t == 12:
                        u = Use(it, "OX")
                        act.wait_ge(work_ready, u.ready)
                        nc.scalar.copy(x2T[:].rearrange("p k s -> p (k s)"), work[u.bank][:]).then_inc(work_free[u.bank], 1)
                        act.wait_ge(work_free[u.bank], u.before + 1)
                        act.sem_inc(x2T_ready, 1)
                    if outs and t == 14:
                        u = Use(it, "R")
                        act.wait_ge(work_ready, u.ready)
                        nc.scalar.copy(r1[:, bass.ds(it.lin(S, -S), S)], work[u.bank][:, 0:S]).then_inc(work_free[u.bank], 1)

            for i in (-1, 0):
                step(Iter(0, i))
            with act.Fori(0, (NB - 2) // 2) as j:
                for r in (1, 2):
                    step(Iter(j, r))
            for i in (NB - 1, NB):
                step(Iter(0, i))

        @block.vector
        def _(dve):
            dve.wait_ge(const_in, 16 * CONST_DMAS)
            dve.wait_ge(ones_set, 3)

            def met():
                dve.sem_inc(dve_met, 1)

            turn = [(d // DH) * DH + (d + DH // 2) % DH for d in range(32)]
            sums_from = [DH + d % DH for d in range(32)]

            def statistics(u, resid, n):
                dve.wait_ge(work_ready, u.ready)
                nc.vector.tensor_tensor(pre[:].rearrange("p t d -> p (t d)"), work[u.bank][:],
                                        resid[:].rearrange("p t d -> p (t d)"), ALU.add).then_inc(work_free[u.bank], 1)
                dve.wait_ge(work_free[u.bank], u.before + 1)
                for t in range(TT):
                    op = nc.vector.bn_stats(stats[:, t, :], pre[:, t, :])
                op.then_inc(ln_chain, 1)
                dve.wait_ge(ln_chain, n * 2 + 1)
                met()
                for t in range(TT):
                    op = nc.vector.bn_aggr(mv[:, t, :], stats[:, t, :])
                op.then_inc(ln_chain, 1)

            def normalise(out, done, n):
                dve.wait_ge(rstd_ready, n + 1)
                for t in range(TT):
                    op = nc.vector.tensor_scalar(out[:, t, :], pre[:, t, :], mv[:, t, 0:1], rstd[:, t:t + 1],
                                                 ALU.subtract, ALU.mult)
                op.then_inc(done, 1)

            def rotated(it, raw, which):
                dve.wait_ge(raw_ready, it.lin(2, 3 + which))
                if which:
                    dve.wait_ge(kr_ready, it.lin(1, 2))
                elif it.at_least(0):
                    dve.wait_ge(qr_ready, it.lin(1, 1))
                met()
                nc.vector.stream_shuffle(rot[:].rearrange("p k s -> p (k s)"), raw[:].rearrange("p k s -> p (k s)"),
                                         turn).then_inc(rot_chain, 1)
                dve.wait_ge(rot_chain, it.lin(2, 3 + which))
                nc.vector.tensor_tensor(rot[:], rot[:], sin[:].unsqueeze(1).to_broadcast([P, KT, S]),
                                        ALU.mult).then_inc(rot_ready, 1)

            def step(it):
                par = (it.r + 1) % 2
                front, outs = it.batch(1), it.batch(-1)
                for t in range(NH):
                    if it.batch(0):
                        dve.wait_ge(score_ready, it.lin(NH, t + 1))
                        if not (it.fixed and it.i == 0 and t < 2):
                            dve.wait_ge(probs_ready, it.lin(NH, t - 1))
                        met()
                        for q in range(TT):
                            op = nc.vector.tensor_tensor_reduce(
                                scored[t % 2][:, q, :], score[t % 2][:, q * S:(q + 1) * S], band[:, q, :],
                                -1.0 / DH ** 0.5, BIG, ALU.add, ALU.min, nmax[t % 2][:, q:q + 1])
                        op.then_inc(scored_ready, 1)
                    if t % 2 == 1 and (it.batch(0) if t >= 3 else it.batch(-1)):
                        dve.wait_ge(turned_ready, it.lin(NH, t - 2))
                        if not (it.fixed and it.i == 0 and t - 3 < NPT):
                            dve.wait_ge(attn_ready, it.lin(NG, (t - 3) // HG - 1))
                        nc.vector.tensor_copy(probsT[(t - 3) % NPT][:].rearrange("p t s -> p (t s)"),
                                              turned[0][:]).then_inc(probsT_even, 1)
                    if t % 4 == 0 and (it.batch(0) if t >= 8 else it.batch(-1)):
                        g = t // 4 - 2
                        bpar = (it.r if g >= 0 else it.r + 1) % 2
                        dve.wait_ge(attn_ready, it.lin(NG, g + 1))
                        if g == 0 and it.at_least(2):
                            dve.wait_ge(work_ready, Use(Iter(it.j, it.r - 1), "O").ready)
                        a = attn[g % 2][:, 0:S]
                        met()
                        nc.vector.stream_shuffle(sums[:], a, sums_from).then_inc(norm_chain, 1)
                        dve.wait_ge(norm_chain, it.lin(2 * NG, 2 * g + 1))
                        nc.vector.reciprocal(sums[:], sums[:]).then_inc(norm_chain, 1)
                        dve.wait_ge(norm_chain, it.lin(2 * NG, 2 * g + 2))
                        nc.vector.tensor_tensor(attnT[bpar][:, g % NG, :], a, sums[:], ALU.mult).then_inc(attnT_ready, 1)
                    if front and t == 1:
                        u = Use(it, "U")
                        dve.wait_ge(work_ready, u.ready)
                        for k in range(KT):
                            op = nc.vector.tensor_tensor_scan(state[:, k, :], acol[:, k:k + 1].to_broadcast([P, S]),
                                                              work[u.bank][:, k * S:(k + 1) * S], 0.0, ALU.mult, ALU.add)
                        op.then_inc(work_free[u.bank], 1)
                        dve.wait_ge(work_free[u.bank], u.before + 1)
                        dve.sem_inc(state_ready, 1)
                    if front and t == 3:
                        rotated(it, raw_k, 0)
                    if front and t == 4:
                        u = Use(it, "V")
                        dve.wait_ge(work_ready, u.ready)
                        if it.at_least(1):
                            dve.wait_ge(attn_ready, it.lin(NG, 0))
                        for k in range(TT):
                            op = nc.vector.tensor_tensor(vp[par][:, k, :, 0:DH],
                                                         work[u.bank][:, k * D:(k + 1) * D].rearrange("p (h d) -> p h d", d=DH),
                                                         bv[:].rearrange("p (h d) -> p h d", d=DH), ALU.add)
                        op.then_inc(work_free[u.bank], 1)
                        dve.wait_ge(work_free[u.bank], u.before + 1)
                        dve.sem_inc(vp_ready, 1)
                    if outs and t == 6:
                        if it.at_least(2):
                            dve.wait_ge(x2_kept, it.lin(1, -1))
                        dve.wait_ge(x1_ready, it.lin(1, 1) if it.batch(0) else NB)
                        statistics(Use(it, "O"), x1[(it.r + 1) % 2], ln_before(it, "O"))
                    if outs and t == 7:
                        normalise(x2cur, x2_ready, ln_before(it, "O"))
                    if front and t == 7:
                        dve.wait_ge(xb_ready, it.lin(1, 2))
                        if outs:
                            dve.wait_ge(x2_ready, it.lin(1, 0))
                        elif it.at_least(0):
                            dve.wait_ge(x1_ready, it.lin(1, 1))
                        statistics(Use(it, "Y"), xb, ln_before(it, "Y"))
                    if front and t == 8:
                        normalise(x1[par], x1_ready, ln_before(it, "Y"))
                    if front and t == 11:
                        rotated(it, raw_q, 1)

            for i in (-1, 0):
                step(Iter(0, i))
            with dve.Fori(0, (NB - 2) // 2) as j:
                for r in (1, 2):
                    step(Iter(j, r))
            for i in (NB - 1, NB):
                step(Iter(0, i))


def routing(nc, dram, keep):
    G = NB * NE // P
    GB = NB // G
    with ExitStack() as ctx:
        def sb(name, *shape, dt=F32):
            return ctx.enter_context(nc.sbuf_tensor(name, [P, *shape], dt))

        def sem(name):
            return ctx.enter_context(nc.semaphore(name))

        r1, x2, acc, ident = keep["r1"], keep["x2"], keep["acc"], keep["ident"]
        token_of, weight_of = keep["token_of"], keep["weight_of"]
        rw2 = sb("rw2", NE)
        rw2_placed = sb("rw2_placed", GB, P)
        p = [sb(f"p{g}", S) for g in range(G)]
        nmax, total = sb("nmaxr", G), sb("total", G)
        top = [sb(f"top{g}", CAP) for g in range(G)]
        where = [sb(f"where{g}", CAP, dt=U32) for g in range(G)]
        token = [sb(f"token{g}", 2, CAP) for g in range(G)]
        weight = [sb(f"weight{g}", 2, CAP) for g in range(G)]
        wsum = sb("wsum", G)
        logits = [ctx.enter_context(nc.psum_tensor(f"logits{g}", [P, 512], F32)) for g in range(G)]
        turned = [ctx.enter_context(nc.psum_tensor(f"turnedr{n}", [P, 512], F32)) for n in range(2 * G)]

        rw2_in, zeroed, placed, silu_done = sem("rw2_in"), sem("zeroed"), sem("placed"), sem("silu_done")
        logits_ready, nmax_ready, exp_done = sem("logits_ready"), sem("nmax_ready"), sem("exp_done")
        chain, picked, rows_turned, tokens_out = sem("chain"), sem("picked"), sem("rows_turned"), sem("tokens_out")
        copied = sem("copied")
        block = ctx.enter_context(nc.Block())

        @block.sync
        def _(sp):
            sp.dma_start(rw2[:], dram["rw2"]).then_inc(rw2_in, 16)
            sp.wait_ge(picked, 1)
            for g in range(G):
                sp.dma_start(dram["tokens"][g * P:(g + 1) * P, :], token[g][:, 0, :]).then_inc(tokens_out, 16)
            sp.wait_ge(tokens_out, 16 * G)

        @block.gpsimd
        def _(pool):
            nc.gpsimd.memset(rw2_placed[:], 0.0).then_inc(zeroed, 1)
            pool.wait_ge(zeroed, 1)
            pool.wait_ge(rw2_in, 16)
            for c in range(GB):
                op = nc.gpsimd.tensor_copy(rw2_placed[:, c, c * NE:(c + 1) * NE], rw2[:])
            op.then_inc(placed, 1)
            for b in range(NB):
                op = nc.gpsimd.tensor_copy(acc[:, b, :], x2[:, b * TT * D:(b + 1) * TT * D])
            op.then_inc(copied, 1)
            pool.wait_ge(copied, 1)

        @block.scalar
        def _(act):
            for g in range(G):
                half = r1[:, g * GB * S:(g + 1) * GB * S]
                nc.scalar.activation(half, half, ACT.Silu).then_inc(silu_done, 1)
            for g in range(G):
                act.wait_ge(nmax_ready, 1)
                nc.scalar.activation(p[g][:], logits[g][:, 0:S], ACT.Exp, bias=nmax[:, g:g + 1],
                                     accum_out=total[:, g:g + 1]).then_inc(exp_done, 1)

        @block.tensor
        def _(pe):
            pe.wait_ge(placed, 1)
            for g in range(G):
                pe.wait_ge(silu_done, g + 1)
                for c in range(GB):
                    b = g * GB + c
                    mm = nc.tensor.matmul(logits[g][:, 0:S], rw2_placed[:, c, :], r1[:, b * S:(b + 1) * S],
                                          start=(c == 0), stop=(c == GB - 1))
                mm.then_inc(logits_ready, 1)
            pe.wait_ge(picked, 1)
            for g in range(G):
                for n, src in enumerate((token, weight)):
                    nc.tensor.transpose(turned[2 * g + n][:, 0:P], src[g][:].rearrange("p a s -> p (a s)"),
                                        ident[:]).then_inc(rows_turned, 1)

        @block.vector
        def _(dve):
            links = [0]

            def link(op):
                links[0] += 1
                op.then_inc(chain, 1)
                dve.wait_ge(chain, links[0])

            dve.wait_ge(logits_ready, G)
            for g in range(G):
                op = nc.vector.tensor_reduce(nmax[:, g:g + 1], logits[g][:, 0:S], AX.X, ALU.max)
            link(op)
            nc.vector.tensor_scalar(nmax[:], nmax[:], -1.0, None, ALU.mult).then_inc(nmax_ready, 1)
            dve.wait_ge(exp_done, G)
            link(nc.vector.reciprocal(total[:], total[:]))
            for g in range(G):
                op = nc.vector.tensor_scalar(p[g][:], p[g][:], total[:, g:g + 1], None, ALU.mult)
            link(op)
            for r in range(CAP // 8):
                cols = slice(8 * r, 8 * r + 8)
                for g in range(G):
                    op = nc.vector.max(top[g][:, cols], p[g][:])
                link(op)
                for g in range(G):
                    nc.vector.max_index(where[g][:, cols], top[g][:, cols], p[g][:])
                    op = nc.vector.match_replace(p[g][:], top[g][:, cols], p[g][:], -1.0)
                link(op)
            for g in range(G):
                for a in range(2):
                    nc.vector.tensor_copy(token[g][:, a, :], where[g][:])
                op = nc.vector.tensor_reduce(wsum[:, g:g + 1], top[g][:], AX.X, ALU.add)
            link(op)
            link(nc.vector.tensor_scalar(wsum[:], wsum[:], 1e-9, None, ALU.add))
            link(nc.vector.reciprocal(wsum[:], wsum[:]))
            for g in range(G):
                for a in range(2):
                    op = nc.vector.tensor_scalar(weight[g][:, a, :], top[g][:], wsum[:, g:g + 1], None, ALU.mult)
            op.then_inc(picked, 1)
            for g in range(G):
                for n, out in enumerate((token_of, weight_of)):
                    dve.wait_ge(rows_turned, 2 * g + n + 1)
                    for e in range(2):
                        half = slice(CAP * e, CAP * e + CAP)
                        src = turned[2 * g + n][half, 0:P].rearrange("p (b j e) -> p j b e", j=PAIRS, e=2)
                        nc.vector.tensor_copy(out[half, :, g * GB:(g + 1) * GB], src[:, :, :, e]).then_inc(chain, 1)
                        links[0] += 1
            dve.wait_ge(chain, links[0])


def experts(nc, dram, keep):
    BB = 4
    BLK = 8
    NBLK = NB // BLK
    W = 2 * CAP
    USES = 2 + NBLK * FT * 2 // 2 + NB // 2
    with ExitStack() as ctx:
        def sb(name, *shape, dt=F32):
            return ctx.enter_context(nc.sbuf_tensor(name, [P, *shape], dt))

        def sem(name):
            return ctx.enter_context(nc.semaphore(name))

        x2, acc, ident = keep["x2"], keep["acc"], keep["ident"]
        token_of, weight_of = keep["token_of"], keep["weight_of"]
        iota_p, iota_f = sb("iota_p", TT), sb("iota_f", S)
        tokens = sb("tokens", NB, W)
        onehot = sb("onehot", TT, NB * W)
        picked = sb("picked_x", KT, 2, NB * CAP)
        w1 = [sb(f"w1_{e}", KT, FF) for e in range(2)]
        w2 = [sb(f"w2_{e}", KT, FF) for e in range(2)]
        w3 = [sb(f"w3_{e}", FT, D) for e in range(2)]
        gate = [sb(f"gate{n}", 512) for n in range(2)]
        hidden = [sb(f"hidden{n}", FT, 512) for n in range(2)]
        yT = sb("yT", KT, NB, 2, CAP)
        y = [sb(f"y{n}", D) for n in range(2)]
        spread = [sb(f"spread{n}", S) for n in range(2)]
        stats, mv, rstd = sb("stats3", NB * TT, 6), sb("mv3", NB * TT, 2), sb("rstd3", NB * TT)
        log, guess, newton = sb("log3", NB * TT), sb("guess3", NB * TT), sb("newton3", NB * TT)
        bank = [ctx.enter_context(nc.psum_tensor(f"bank{n}", [P, 512], F32)) for n in range(4)]
        ybank = [ctx.enter_context(nc.psum_tensor(f"ybank{n}", [P, 512], F32)) for n in range(2)]

        iota_in, tokens_in, tokens_read = sem("iota_in"), sem("tokens_in"), sem("tokens_read")
        weights_in = [sem(f"weights_in{e}") for e in range(2)]
        free = [sem(f"free{n}") for n in range(4)]
        yfree = [sem(f"yfree{n}") for n in range(2)]
        onehot_ready, gathered, picked_ready = sem("onehot_ready"), sem("gathered"), sem("picked_ready")
        product_ready, gate_ready, hidden_ready = sem("product_ready"), sem("gate_ready"), sem("hidden_ready")
        y_ready, turned_ready, y_scaled = sem("y_ready"), sem("turned_ready3"), sem("y_scaled")
        spread_ready, added_ready, added = sem("spread_ready"), sem("added_ready"), sem("added")
        log_chain, guess_ready, newton_chain = sem("log_chain3"), sem("guess_ready3"), sem("newton_chain3")
        ln, rstd_ready, ln_done, out_done = sem("ln"), sem("rstd_ready3"), sem("ln_done"), sem("out_done")
        GU = NB // BB * KT
        FU = 2 * NBLK * FT
        YU = 2 * NBLK * KT

        block = ctx.enter_context(nc.Block())

        @block.sync
        def _(sp):
            sp.dma_start(iota_p[:], dram["iota_p"]).then_inc(iota_in, 16)
            sp.dma_start(iota_f[:], dram["iota_f"].partition_broadcast(P)).then_inc(iota_in, 16)

            def load(j, first):
                if not first:
                    sp.wait_ge(tokens_read, j)
                src = dram["tokens"].rearrange("(b e) s -> b (e s)", e=NE)[:, bass.ds(j * W, W)]
                sp.dma_start(tokens[:], src.partition_broadcast(P)).then_inc(tokens_in, 16)
                for e in range(2):
                    if not first:
                        sp.wait_ge(y_ready, j * YU + (e + 1) * YU // 2 - YU)
                    ex = j * 2 + e
                    sp.dma_start(w1[e][:], dram["w1"][bass.ds(ex, 1)].rearrange("o (k p) f -> p (o k) f", p=P)).then_inc(weights_in[e], 16)
                    sp.dma_start(w2[e][:], dram["w2"][bass.ds(ex, 1)].rearrange("o (k p) f -> p (o k) f", p=P)).then_inc(weights_in[e], 16)
                    sp.dma_start(w3[e][:], dram["w3"][bass.ds(ex, 1)].rearrange("o (k p) d -> p (o k) d", p=P)).then_inc(weights_in[e], 16)

            load(0, True)
            with sp.Fori(1, PAIRS) as j:
                load(j, False)
            for b in range(NB):
                sp.wait_ge(ln_done, b + 1)
                sp.dma_start(dram["out"][b].rearrange("(t p) d -> p t d", p=P),
                             acc[:, b, :].rearrange("p (t d) -> p t d", t=TT)).then_inc(out_done, 16)
            sp.wait_ge(out_done, 16 * NB)

        @block.gpsimd
        def _(pool):
            pool.wait_ge(guess_ready, 1)
            refine_deviation(pool, lambda: None, mv[:, :, 1], guess[:], newton[:], rstd[:], newton_chain, 0, rstd_ready)

        @block.tensor
        def _(pe):
            def pair(j):
                used = [0] * 4

                def take(n):
                    pe.wait_ge(free[n], j * USES + used[n])
                    used[n] += 1
                    return bank[n]

                pe.wait_ge(onehot_ready, j + 1)
                u = 0
                for q in range(NB // BB):
                    for k in range(KT):
                        w = take(u % 4)
                        for c in range(BB):
                            b = q * BB + c
                            for t in range(TT):
                                at = (b * TT + t) * D + k * P
                                mm = nc.tensor.matmul(w[:, c * W:(c + 1) * W], x2[:, at:at + P],
                                                      onehot[:, t, b * W:(b + 1) * W],
                                                      start=(t == 0), stop=(t == TT - 1))
                        mm.then_inc(gathered, 1)
                        u += 1
                n = 0
                for e in range(2):
                    pe.wait_ge(weights_in[e], j * 48 + 48)
                    for blk in range(NBLK):
                        cols = slice(blk * 512, blk * 512 + 512)
                        pe.wait_ge(picked_ready, j * GU + (blk + 1) * GU // NBLK)
                        for f in range(FT):
                            wg, wv = take(f % 2 * 2), take(f % 2 * 2 + 1)
                            for k in range(KT):
                                nc.tensor.matmul(wg[:], w1[e][:, k, f * P:(f + 1) * P], picked[:, k, e, cols],
                                                 start=(k == 0), stop=(k == KT - 1))
                            for k in range(KT):
                                mm = nc.tensor.matmul(wv[:], w2[e][:, k, f * P:(f + 1) * P], picked[:, k, e, cols],
                                                      start=(k == 0), stop=(k == KT - 1))
                            mm.then_inc(product_ready, 1)
                        s = 2 * e + blk
                        for k in range(KT):
                            pe.wait_ge(yfree[k], j * (YU // KT) + s)
                            for f in range(FT):
                                pe.wait_ge(hidden_ready, j * FU + s * FT + f + 1)
                                mm = nc.tensor.matmul(ybank[k][:], w3[e][:, f, k * P:(k + 1) * P],
                                                      hidden[s % 2][:, f, :], start=(f == 0), stop=(f == FT - 1))
                            mm.then_inc(y_ready, 1)
                for b in range(NB + 1):
                    if b < NB:
                        w = take(b % 2)
                        if b == 0:
                            for k in range(KT):
                                pe.wait_ge(yfree[k], j * (YU // KT) + YU // KT)
                        for k in range(KT):
                            mm = nc.tensor.transpose(w[:, k * P:(k + 1) * P],
                                                     yT[:, k, b, :, :].rearrange("p e s -> p (e s)"), ident[:])
                        mm.then_inc(turned_ready, 1)
                    if b > 0:
                        c = b - 1
                        w = take(2 + c % 2)
                        pe.wait_ge(y_scaled, j * NB + c + 1)
                        pe.wait_ge(spread_ready, j * NB + c + 1)
                        for t in range(TT):
                            mm = nc.tensor.matmul(w[:, t * D:(t + 1) * D], spread[c % 2][:, t * P:(t + 1) * P],
                                                  y[c % 2][:], start=True, stop=True)
                        mm.then_inc(added_ready, 1)

            with pe.Fori(0, PAIRS) as j:
                pair(j)

        @block.scalar
        def _(act):
            act.wait_ge(iota_in, 32)

            def pair(j):
                u = 0
                for q in range(NB // BB):
                    for k in range(KT):
                        act.wait_ge(gathered, j * GU + u + 1)
                        dst = picked[:, k, :, q * BB * CAP:(q + 1) * BB * CAP].rearrange("p e (b s) -> p b e s", s=CAP)
                        nc.scalar.copy(dst, bank[u % 4][:].rearrange("p (b e s) -> p b e s", b=BB, e=2)).then_inc(free[u % 4], 1)
                        act.wait_ge(free[u % 4], j * USES + u // 4 + 1)
                        act.sem_inc(picked_ready, 1)
                        u += 1
                for s in range(2 * NBLK):
                    for f in range(FT):
                        n = s * FT + f
                        act.wait_ge(product_ready, j * FU + n + 1)
                        if n >= 2:
                            act.wait_ge(hidden_ready, j * FU + n - 1)
                        a = nc.scalar.activation(gate[f % 2][:], bank[f % 2 * 2][:], ACT.Silu)
                        a.then_inc(free[f % 2 * 2], 1)
                        act.wait_ge(free[f % 2 * 2], j * USES + 2 + n // 2 + 1)
                        act.sem_inc(gate_ready, 1)
                    for k in range(KT):
                        act.wait_ge(y_ready, j * YU + s * KT + k + 1)
                        e, blk = s // NBLK, s % NBLK
                        nc.scalar.copy(yT[:, k, blk * BLK:(blk + 1) * BLK, e, :],
                                       ybank[k][:].rearrange("p (b s) -> p b s", s=CAP)).then_inc(yfree[k], 1)
                for b in range(NB):
                    act.wait_ge(turned_ready, j * NB + b + 1)
                    if b >= 2:
                        act.wait_ge(added_ready, j * NB + b - 1)
                    nc.scalar.activation(y[b % 2][:], bank[b % 2][:, 0:D], ACT.Copy,
                                         scale=weight_of[:, bass.ds(j, 1), b]).then_inc(free[b % 2], 1)
                    act.wait_ge(free[b % 2], j * USES + 2 + FU // 2 + b // 2 + 1)
                    act.sem_inc(y_scaled, 1)

            with act.Fori(0, PAIRS) as j:
                pair(j)
            act.wait_ge(ln, 2)
            estimate_deviation(act, mv[:, :, 1], log[:], guess[:], log_chain, 0, guess_ready)

        @block.vector
        def _(dve):
            dve.wait_ge(iota_in, 32)

            def build(j):
                dve.wait_ge(tokens_in, j * 16 + 16)
                for t in range(TT):
                    op = nc.vector.tensor_scalar(onehot[:, t, :], tokens[:].rearrange("p b w -> p (b w)"),
                                                 iota_p[:, t:t + 1], None, ALU.is_equal)
                op.then_inc(onehot_ready, 1)

            def pair(j, last):
                for s in range(2 * NBLK):
                    for f in range(FT):
                        n = s * FT + f
                        dve.wait_ge(gate_ready, j * FU + n + 1)
                        if f == 0 and s >= 2:
                            dve.wait_ge(y_ready, j * YU + (s - 1) * KT)
                        nc.vector.tensor_tensor(hidden[s % 2][:, f, :], gate[f % 2][:], bank[f % 2 * 2 + 1][:],
                                                ALU.mult).then_inc(hidden_ready, 1)
                        dve.wait_ge(hidden_ready, j * FU + n + 1)
                        dve.sem_inc(free[f % 2 * 2 + 1], 1)
                    if s == 0:
                        dve.wait_ge(onehot_ready, j + 1)
                        dve.sem_inc(tokens_read, 1)
                        if not last:
                            dve.wait_ge(gathered, j * GU + GU)
                            build(j + 1)
                for b in range(NB + 1):
                    if b < NB:
                        if b >= 2:
                            dve.wait_ge(added_ready, j * NB + b - 1)
                        nc.vector.tensor_scalar(spread[b % 2][:], iota_f[:], token_of[:, bass.ds(j, 1), b], None,
                                                ALU.is_equal).then_inc(spread_ready, 1)
                    if b > 0:
                        c = b - 1
                        dve.wait_ge(added_ready, j * NB + c + 1)
                        nc.vector.tensor_tensor(acc[:, c, :], acc[:, c, :], bank[2 + c % 2][:],
                                                ALU.add).then_inc(free[2 + c % 2], 1)

            build(0)
            with dve.Fori(0, PAIRS - 1) as j:
                pair(j, False)
            pair(PAIRS - 1, True)
            dve.wait_ge(free[2], PAIRS * USES)
            dve.wait_ge(free[3], PAIRS * USES)
            for b in range(NB):
                for t in range(TT):
                    op = nc.vector.bn_stats(stats[:, b * TT + t, :], acc[:, b, t * D:(t + 1) * D])
            op.then_inc(ln, 1)
            dve.wait_ge(ln, 1)
            for n in range(NB * TT):
                op = nc.vector.bn_aggr(mv[:, n, :], stats[:, n, :])
            op.then_inc(ln, 1)
            dve.wait_ge(ln, 2)
            dve.wait_ge(rstd_ready, 1)
            for b in range(NB):
                for t in range(TT):
                    n = b * TT + t
                    op = nc.vector.tensor_scalar(acc[:, b, t * D:(t + 1) * D], acc[:, b, t * D:(t + 1) * D],
                                                 mv[:, n, 0:1], rstd[:, n:n + 1], ALU.subtract, ALU.mult)
                op.then_inc(ln_done, 1)


def program(nc, dram):
    with ExitStack() as ctx:
        def sb(name, *shape):
            return ctx.enter_context(nc.sbuf_tensor(name, [P, *shape], F32))

        keep = {"x2": sb("x2", NB * TT * D), "ident": sb("ident", P)}
        with nc.sbuf_tensor("r1", [P, NB * S], F32) as r1:
            keep["r1"] = r1
            mixing(nc, dram, keep)
            with ExitStack() as later:
                for name, shape in (("acc", [P, NB, TT * D]), ("token_of", [P, PAIRS, NB]), ("weight_of", [P, PAIRS, NB])):
                    keep[name] = later.enter_context(nc.sbuf_tensor(name, shape, F32))
                routing(nc, dram, keep)
                experts(nc, dram, keep)


def kernel(**inputs):
    import numpy as np
    import concourse.bacc as bacc
    from concourse.bass_utils import run_bass_kernel_spmd

    a = {k: np.asarray(v) for k, v in inputs.items()}
    c = np.ascontiguousarray
    arrays = {
        "x": c(a["x"]), "xT": c(a["x"].transpose(0, 2, 1)), "cT": c(a["ctx_1024"].transpose(0, 2, 1)),
        "mix_A": c(a["L0_attn_A"].reshape(KT, P).T), "mix_BT": c(a["L0_attn_B"].T), "mix_WT": c(a["L0_attn_W"].T), "mix_b": c(a["L0_attn_b"]),
        "WqT": c(a["L0_xattn_Wq"].T), "bq": c(a["L0_xattn_bq"].reshape(KT, P).T), "WkT": c(a["L0_xattn_Wk"].T), "bk": c(a["L0_xattn_bk"].reshape(KT, P).T),
        "WvT": c(a["L0_xattn_Wv"].T), "bv": c(a["L0_xattn_bv"]), "WoT": c(a["L0_xattn_Wo"].T), "bo": c(a["L0_xattn_bo"]),
        "rw1": c(a["L0_ffn_router_w1"]), "rw2": c(a["L0_ffn_router_w2"]),
        "w1": c(a["L0_ffn_w1"]), "w2": c(a["L0_ffn_w2"]), "w3": c(a["L0_ffn_w3"]),
    }
    rows = np.arange(P)
    freq = (np.float32(1.0) / np.power(np.float32(10000.0), np.arange(0, DH, 2, dtype=np.float32) / np.float32(DH))).astype(np.float32)
    angle = (freq[rows % (DH // 2)][:, None] * np.arange(S, dtype=np.float32)[None, :]).astype(np.float32)
    sign = np.where(rows % DH < DH // 2, -1.0, 1.0)[:, None]
    pos = np.arange(S)
    arrays["cos"] = np.cos(angle.astype(np.float64)).astype(np.float32)
    arrays["sin"] = (sign * np.sin(angle.astype(np.float64))).astype(np.float32)
    arrays["band"] = np.where(np.abs(pos[:, None] - pos[None, :]) <= WINDOW, 0.0, MASKED).astype(np.float32)
    arrays["head_rows"] = (rows[:, None] // DH == np.arange(HPT)[None, :]).astype(np.float32)
    arrays["ident"] = np.eye(P, dtype=np.float32)
    arrays["iota_p"] = (rows[:, None] + P * np.arange(TT)[None, :]).astype(np.float32)
    arrays["iota_f"] = np.arange(S, dtype=np.float32)

    nc = bacc.Bacc("TRN2", target_bir_lowering=False, num_devices=1)
    dram = {k: nc.dram_tensor(f"in_{k}", v.shape, F32, kind="ExternalInput").ap() for k, v in arrays.items()}
    dram["tokens"] = nc.dram_tensor("tokens_scratch", (NB * NE, CAP), F32, kind="Internal").ap()
    dram["out"] = nc.dram_tensor("out_0", (NB, S, D), F32, kind="ExternalOutput").ap()
    program(nc, dram)
    r = run_bass_kernel_spmd(nc, [{f"in_{k}": v for k, v in arrays.items()}], core_ids=[0])
    return r.results[0]["out_0"]
```

```python
from contextlib import ExitStack

import concourse.bass as bass
from concourse import mybir

F32 = mybir.dt.float32
F32R = mybir.dt.float32r
U32 = mybir.dt.uint32
ALU = mybir.AluOpType
ACT = mybir.ActivationFunctionType
AX = mybir.AxisListType

P = 128
NB = 16
S = 256
D = 256
KT = D // P
TT = S // P
NH = 16
DH = D // NH
HG = 4
NG = NH // HG
HPT = P // DH
WINDOW = 50
HID = 128
NE = 16
CAP = 64
FF = 512
FT = FF // P
NC2 = NB // 2
EPS = 1e-5
MASKED = -4e9
BIG = 3e38


class Iter:

    def __init__(self, j, r):
        self.j, self.r = j, r
        self.fixed = isinstance(j, int)
        self.i = 2 * j + r

    def lin(self, a, c):
        return self.j * (2 * a) + (a * self.r + c)

    def half(self, a, c):
        return self.j * a + (a * self.r + c) // 2

    def loads(self, d):
        return self.j * 48 + 48 * ((self.r + d) // 2 + 1)

    def batch(self, d):
        return not self.fixed or 0 <= self.i + d < NB

    def at_least(self, n):
        return not self.fixed or self.i >= n


FULL = ["U", "K", "V", "O", "Y", "X", "Q", "OX", "R"]
FRONT = [n for n in FULL if n not in ("O", "OX", "R")]
OUTS = ["O", "OX", "R"]
NF, NFR, NO = len(FULL), len(FRONT), len(OUTS)


class Use:

    def __init__(self, it, name):
        if it.fixed and it.i == -1:
            n = FRONT.index(name)
        elif it.fixed and it.i == 0:
            n = NFR + FRONT.index(name)
        elif it.fixed and it.i >= NB - 1:
            n = 2 * NFR + NF * (NB - 2) + NO * (it.i - NB + 1) + OUTS.index(name)
        else:
            c = 2 * NFR - NF + FULL.index(name)
            self.bank = (NF * it.r + c) % 2
            self.ready = it.lin(NF, c + 1)
            self.before = it.half(NF, c)
            self.first = False
            return
        self.bank, self.ready, self.before, self.first = n % 2, n + 1, n // 2, n < 2


def estimate_deviation(act, var, log, guess, chain, before, ready):
    act.activation(log, var, ACT.Ln, bias=EPS).then_inc(chain, 1)
    act.wait_ge(chain, before + 1)
    act.activation(guess, log, ACT.Exp, scale=-0.5).then_inc(ready, 1)


def refine_deviation(pool, met, var, guess, tmp, rstd, chain, before, ready):
    met()
    pool.tensor_scalar(rstd, var, EPS, None, ALU.add)
    pool.tensor_tensor(tmp, guess, guess, ALU.mult).then_inc(chain, 1)
    pool.wait_ge(chain, before + 1)
    pool.tensor_tensor(tmp, tmp, rstd, ALU.mult).then_inc(chain, 1)
    pool.wait_ge(chain, before + 2)
    met()
    pool.tensor_scalar(tmp, tmp, -0.5, 1.5, ALU.mult, ALU.add).then_inc(chain, 1)
    pool.wait_ge(chain, before + 3)
    pool.tensor_tensor(rstd, guess, tmp, ALU.mult).then_inc(ready, 1)


def ln_before(it, name):
    if it.fixed and it.i < 1:
        return it.i + 1
    if it.fixed and it.i >= NB:
        return 2 * NB - 1
    return it.lin(2, 0 if name == "O" else 1)


def mixing(nc, dram, keep):
    with ExitStack() as ctx:
        def sb(name, *shape):
            return ctx.enter_context(nc.sbuf_tensor(name, [P, *shape], F32))

        def ps(name):
            return ctx.enter_context(nc.psum_tensor(name, [P, 512], F32))

        def sem(name):
            return ctx.enter_context(nc.semaphore(name))

        r1 = keep["r1"]
        ident = keep["ident"]
        wb, ww = sb("wb", KT, D), sb("ww", KT, D)
        wq, wk, wv = sb("wq", KT, D), sb("wk", KT, D), sb("wv", KT, D)
        wo = sb("wo", NG, D)
        rw1 = sb("rw1", KT, HID)
        cos, sin = sb("cos", S), sb("sin", S)
        band = sb("band", TT, S)
        head_rows = sb("head_rows", HPT)
        acol, bq, bk = sb("acol", KT), sb("bq", KT), sb("bk", KT)
        b_mix, bv = sb("b_mix", D), sb("bv", D)
        xT = [sb(f"xT{n}", KT, S) for n in range(2)]
        cT = [sb(f"cT{n}", KT, S) for n in range(2)]
        xin = [sb(f"xin{n}", TT, D) for n in range(2)]
        state = sb("state", KT, S)
        xb = sb("xb", TT, D)
        pre = sb("pre", TT, D)
        stats, mv, rstd = sb("stats", TT, 6), sb("mv", TT, 2), sb("rstd", TT)
        log, guess, newton = sb("log", TT), sb("guess", TT), sb("newton", TT)
        x1 = [sb(f"x1_{n}", TT, D) for n in range(2)]
        x1T = sb("x1T", KT, S)
        raw_q, raw_k = sb("raw_q", KT, S), sb("raw_k", KT, S)
        rot = sb("rot", KT, S)
        rope = sb("rope", KT, S)
        kr = [sb(f"kr{n}", KT, S) for n in range(2)]
        qm = [sb(f"qm{n}", NH, S) for n in range(2)]
        vp = [sb(f"vp{n}", TT, NH, 2 * DH) for n in range(2)]
        scored = [sb(f"scored{n}", TT, S) for n in range(2)]
        nmax = [sb(f"nmax{n}", TT) for n in range(2)]
        probs = [sb(f"probs{n}", TT, S) for n in range(2)]
        NPT = 8
        probsT = [sb(f"probsT{n}", TT, S) for n in range(NPT)]
        sums = sb("sums", S)
        attnT = [sb(f"attnT{n}", NG, S) for n in range(2)]
        x2cur = sb("x2cur", TT, D)
        x2T = sb("x2T", KT, S)

        work = [ps(f"work{n}") for n in range(2)]
        score = [ps(f"score{n}") for n in range(2)]
        turned = [ps(f"turned{n}") for n in range(2)]
        attn = [ps(f"attn{n}") for n in range(2)]

        dve_met, pool_met = sem("dve_met"), sem("pool_met")
        const_in = sem("const_in")
        batch_in = [sem(f"batch_in{n}") for n in range(2)]
        ones_set = sem("ones_set")
        work_ready = sem("work_ready")
        work_free = [sem(f"work_free{n}") for n in range(2)]
        xb_ready = sem("xb_ready")
        state_ready = sem("state_ready")
        log_chain, guess_ready, newton_chain, rstd_ready = sem("log_chain"), sem("guess_ready"), sem("newton_chain"), sem("rstd_ready")
        ln_chain, norm_chain, rope_chain = sem("ln_chain"), sem("norm_chain"), sem("rope_chain")
        x1_ready, x1T_ready = sem("x1_ready"), sem("x1T_ready")
        raw_ready, rot_chain, rot_ready = sem("raw_ready"), sem("rot_chain"), sem("rot_ready")
        kr_ready, qr_ready, qm_ready = sem("kr_ready"), sem("qr_ready"), sem("qm_ready")
        vp_ready = sem("vp_ready")
        score_ready, scored_ready = sem("score_ready"), sem("scored_ready")
        probs_ready, turned_ready = sem("probs_ready"), sem("turned_ready")
        probsT_even, probsT_odd = sem("probsT_even"), sem("probsT_odd")
        attn_ready, attnT_ready = sem("attn_ready"), sem("attnT_ready")
        x2_ready, x2_kept, x2T_ready = sem("x2_ready"), sem("x2_kept"), sem("x2T_ready")

        consts = [
            (wb, dram["mix_BT"].rearrange("(k p) n -> p k n", p=P)),
            (ww, dram["mix_WT"].rearrange("(k p) n -> p k n", p=P)),
            (wq, dram["WqT"].rearrange("(k p) n -> p k n", p=P)),
            (wk, dram["WkT"].rearrange("(k p) n -> p k n", p=P)),
            (wv, dram["WvT"].rearrange("(k p) n -> p k n", p=P)),
            (rw1, dram["rw1"].rearrange("(k p) n -> p k n", p=P)),
            (cos, dram["cos"]), (sin, dram["sin"]),
            (band, dram["band"].rearrange("(t p) k -> p t k", p=P)),
            (head_rows, dram["head_rows"]), (ident, dram["ident"]),
            (acol, dram["mix_A"]),
            (bq, dram["bq"]),
            (bk, dram["bk"]),
            (b_mix, dram["mix_b"].partition_broadcast(P)),
            (bv, dram["bv"].partition_broadcast(P)),
        ]
        wo_rows = dram["WoT"].rearrange("(g q d) n -> q d g n", g=NG, q=HG)
        CONST_DMAS = len(consts) + HG + 1

        block = ctx.enter_context(nc.Block())

        @block.sync
        def _(sp):
            def load(par, b):
                sp.dma_start(xT[par][:], dram["xT"][b].rearrange("(k p) s -> p k s", p=P)).then_inc(batch_in[par], 16)
                sp.dma_start(cT[par][:], dram["cT"][b].rearrange("(k p) s -> p k s", p=P)).then_inc(batch_in[par], 16)
                sp.dma_start(xin[par][:], dram["x"][b].rearrange("(t p) d -> p t d", p=P)).then_inc(batch_in[par], 16)

            load(0, 0)
            for tile, src in consts:
                sp.dma_start(tile[:], src).then_inc(const_in, 16)
            sp.wait_ge(ones_set, 3)
            for q in range(HG):
                sp.dma_start(wo[32 * q:32 * q + DH, :, :], wo_rows[q]).then_inc(const_in, 16)
            sp.dma_start(wo[DH:DH + 1, 0, :], dram["bo"].partition_broadcast(1)).then_inc(const_in, 16)
            load(1, 1)
            for b in (2, 3):
                sp.wait_ge(work_ready, Use(Iter(0, b - 3), "V").ready)
                sp.wait_ge(xb_ready, b - 1)
                load(b % 2, b)
            with sp.Fori(0, (NB - 4) // 2) as j:
                for r in range(2):
                    b = j * 2 + (4 + r)
                    sp.wait_ge(work_ready, Use(Iter(j, r + 1), "V").ready)
                    sp.wait_ge(xb_ready, b - 1)
                    load(r, b)

        @block.gpsimd
        def _(pool):
            nc.gpsimd.memset(wo[:], 0.0).then_inc(ones_set, 1)
            for n in range(2):
                nc.gpsimd.memset(vp[n][:], 1.0).then_inc(ones_set, 1)
            pool.wait_ge(const_in, 16 * CONST_DMAS)

            def rotate(it, raw, out, done, which):
                pool.wait_ge(raw_ready, it.lin(2, 3 + which))
                pool_mul = nc.gpsimd.tensor_tensor(rope[:], raw[:], cos[:].unsqueeze(1).to_broadcast([P, KT, S]), ALU.mult)
                pool_mul.then_inc(rope_chain, 1)
                pool.wait_ge(rope_chain, it.lin(2, 3 + which))
                pool.wait_ge(rot_ready, it.lin(2, 3 + which))
                nc.gpsimd.tensor_tensor(out[:], rope[:], rot[:], ALU.add).then_inc(done, 1)

            def met():
                pool.sem_inc(pool_met, 1)

            def inverse_deviation(n):
                pool.wait_ge(guess_ready, n + 1)
                refine_deviation(pool, met, mv[:, :, 1], guess[:], newton[:], rstd[:], newton_chain, n * 3, rstd_ready)

            def step(it):
                par = (it.r + 1) % 2
                front, outs = it.batch(1), it.batch(-1)
                if front:
                    pool.wait_ge(batch_in[par], it.loads(1))
                    if it.at_least(0):
                        pool.wait_ge(x1_ready, it.lin(1, 1))
                    nc.gpsimd.tensor_tensor(xb[:], xin[par][:], b_mix[:].unsqueeze(1).to_broadcast([P, TT, D]),
                                            ALU.add).then_inc(xb_ready, 1)
                    if it.at_least(1):
                        pool.wait_ge(score_ready, it.lin(NH, 0))
                    rotate(it, raw_k, kr[par], kr_ready, 0)
                if outs:
                    inverse_deviation(ln_before(it, "O"))
                if front:
                    inverse_deviation(ln_before(it, "Y"))
                    rotate(it, raw_q, raw_q, qr_ready, 1)
                    pool.wait_ge(qr_ready, it.lin(1, 2))
                    met()
                    for h in range(NH):
                        nc.gpsimd.tensor_scalar(qm[par][:, h, :], raw_q[:, h // HPT, :],
                                                head_rows[:, h % HPT:h % HPT + 1], None,
                                                ALU.mult).then_inc(qm_ready, 1)

            for i in (-1, 0):
                step(Iter(0, i))
            with pool.Fori(0, (NB - 2) // 2) as j:
                for r in (1, 2):
                    step(Iter(j, r))
            for i in (NB - 1, NB):
                step(Iter(0, i))

        @block.tensor
        def _(pe):
            pe.wait_ge(const_in, 16 * CONST_DMAS)

            def begin(u):
                if not u.first:
                    pe.wait_ge(work_free[u.bank], u.before)
                return work[u.bank]

            def heads(it, t):
                if it.batch(0):
                    if not (it.fixed and it.i == 0 and t < 2):
                        pe.wait_ge(scored_ready, it.lin(NH, t - 1))
                    if t == 0:
                        pe.wait_ge(kr_ready, it.lin(1, 1))
                    pe.wait_ge(qm_ready, it.lin(NH, t + 1))
                    for q in range(TT):
                        mm = nc.tensor.matmul(score[t % 2][:, q * S:(q + 1) * S],
                                              qm[it.r % 2][:, t, q * P:(q + 1) * P],
                                              kr[it.r % 2][:, t // HPT, :], start=True, stop=True)
                    mm.then_inc(score_ready, 1)
                if it.batch(0) if t >= 2 else it.batch(-1):
                    pe.wait_ge(probs_ready, it.lin(NH, t - 1))
                    if not (it.fixed and it.i == 0 and t < 4):
                        pe.wait_ge(probsT_odd if t % 2 else probsT_even, it.half(NH, t - 2))
                    for q in range(TT):
                        for k in range(TT):
                            mm = nc.tensor.transpose(turned[t % 2][:, k * S + q * P:k * S + (q + 1) * P],
                                                     probs[t % 2][:, q, k * P:(k + 1) * P], ident[:])
                    mm.then_inc(turned_ready, 1)
                if t % 4 == 3 and (it.batch(0) if t >= 7 else it.batch(-1)):
                    g = (t - 7) // 4
                    vpar = (it.r if g >= 0 else it.r + 1) % 2
                    pe.wait_ge(probsT_even, it.lin(2 * NG, 2 * (g + 1)))
                    pe.wait_ge(probsT_odd, it.lin(2 * NG, 2 * (g + 1)))
                    pe.wait_ge(vp_ready, it.lin(1, 1 if g >= 0 else 0))
                    if not (it.fixed and it.i == 0 and g < 2):
                        pe.wait_ge(attnT_ready, it.lin(NG, g - 1))
                    for k in range(TT):
                        for q in range(HG):
                            h = HG * (g % NG) + q
                            mm = nc.tensor.matmul(attn[g % 2][32 * q:32 * q + 32, 0:S], vp[vpar][:, k, h, :],
                                                  probsT[(HG * g + q) % NPT][:, k, :],
                                                  start=(k == 0), stop=(k == TT - 1))
                    mm.then_inc(attn_ready, 1)

            def step(it):
                par = (it.r + 1) % 2
                front, outs = it.batch(1), it.batch(-1)
                for t in range(NH):
                    heads(it, t)
                    if front and t == 0:
                        u = Use(it, "U")
                        pe.wait_ge(batch_in[par], it.loads(1))
                        w = begin(u)
                        for n in range(KT):
                            for k in range(KT):
                                mm = nc.tensor.matmul(w[:, n * S:(n + 1) * S], wb[:, k, n * P:(n + 1) * P],
                                                      xT[par][:, k, :], start=(k == 0), stop=(k == KT - 1))
                        mm.then_inc(work_ready, 1)
                    if front and t == 1:
                        w = begin(Use(it, "K"))
                        for n in range(KT):
                            for k in range(KT):
                                mm = nc.tensor.matmul(w[:, n * S:(n + 1) * S], wk[:, k, n * P:(n + 1) * P],
                                                      cT[par][:, k, :], start=(k == 0), stop=(k == KT - 1))
                        mm.then_inc(work_ready, 1)
                    if front and t == 2:
                        w = begin(Use(it, "V"))
                        for n in range(TT):
                            for k in range(KT):
                                mm = nc.tensor.matmul(w[:, n * D:(n + 1) * D], cT[par][:, k, n * P:(n + 1) * P],
                                                      wv[:, k, :], start=(k == 0), stop=(k == KT - 1))
                        mm.then_inc(work_ready, 1)
                    if outs and t == 5:
                        w = begin(Use(it, "O"))
                        pe.wait_ge(attnT_ready, it.lin(NG, 0))
                        for n in range(TT):
                            for g in range(NG):
                                mm = nc.tensor.matmul(w[:, n * D:(n + 1) * D], attnT[(it.r + 1) % 2][:, g, n * P:(n + 1) * P],
                                                      wo[:, g, :], start=(g == 0), stop=(g == NG - 1))
                        mm.then_inc(work_ready, 1)
                    if front and t == 6:
                        w = begin(Use(it, "Y"))
                        pe.wait_ge(state_ready, it.lin(1, 2))
                        for n in range(TT):
                            for k in range(KT):
                                mm = nc.tensor.matmul(w[:, n * D:(n + 1) * D], state[:, k, n * P:(n + 1) * P],
                                                      ww[:, k, :], start=(k == 0), stop=(k == KT - 1))
                        mm.then_inc(work_ready, 1)
                    if front and t == 8:
                        w = begin(Use(it, "X"))
                        pe.wait_ge(x1_ready, it.lin(1, 2))
                        for k in range(KT):
                            for n in range(TT):
                                mm = nc.tensor.transpose(w[:, k * S + n * P:k * S + (n + 1) * P],
                                                         x1[par][:, n, k * P:(k + 1) * P], ident[:])
                        mm.then_inc(work_ready, 1)
                    if front and t == 9:
                        w = begin(Use(it, "Q"))
                        pe.wait_ge(x1T_ready, it.lin(1, 2))
                        for n in range(KT):
                            for k in range(KT):
                                mm = nc.tensor.matmul(w[:, n * S:(n + 1) * S], wq[:, k, n * P:(n + 1) * P],
                                                      x1T[:, k, :], start=(k == 0), stop=(k == KT - 1))
                        mm.then_inc(work_ready, 1)
                    if outs and t == 11:
                        w = begin(Use(it, "OX"))
                        pe.wait_ge(x2_ready, it.lin(1, 0))
                        for k in range(KT):
                            for n in range(TT):
                                mm = nc.tensor.transpose(w[:, k * S + n * P:k * S + (n + 1) * P],
                                                         x2cur[:, n, k * P:(k + 1) * P], ident[:])
                        mm.then_inc(work_ready, 1)
                    if outs and t == 13:
                        w = begin(Use(it, "R"))
                        pe.wait_ge(x2T_ready, it.lin(1, 0))
                        for k in range(KT):
                            mm = nc.tensor.matmul(w[:, 0:S], rw1[:, k, :], x2T[:, k, :],
                                                  start=(k == 0), stop=(k == KT - 1))
                        mm.then_inc(work_ready, 1)

            for i in (-1, 0):
                step(Iter(0, i))
            with pe.Fori(0, (NB - 2) // 2) as j:
                for r in (1, 2):
                    step(Iter(j, r))
            for i in (NB - 1, NB):
                step(Iter(0, i))

        @block.scalar
        def _(act):
            act.wait_ge(const_in, 16 * CONST_DMAS)
            act.preload_act_table_set("natural_log_exp_and_others")

            def step(it):
                front, outs = it.batch(1), it.batch(-1)
                for t in range(NH):
                    if it.batch(0):
                        act.wait_ge(scored_ready, it.lin(NH, t + 1))
                        if not (it.fixed and it.i == 0 and t < 2):
                            act.wait_ge(turned_ready, it.lin(NH, t - 1))
                        for q in range(TT):
                            a = nc.scalar.activation(probs[t % 2][:, q, :], scored[t % 2][:, q, :], ACT.Exp,
                                                     bias=nmax[t % 2][:, q:q + 1], scale=-1.0)
                        a.then_inc(probs_ready, 1)
                    if t % 2 == 0 and (it.batch(0) if t >= 3 else it.batch(-1)):
                        act.wait_ge(turned_ready, it.lin(NH, t - 2))
                        if not (it.fixed and it.i == 0 and t - 3 < NPT):
                            act.wait_ge(attn_ready, it.lin(NG, (t - 3) // HG - 1))
                        nc.scalar.copy(probsT[(t - 3) % NPT][:].rearrange("p t s -> p (t s)"),
                                       turned[1][:]).then_inc(probsT_odd, 1)
                    for when, name, raw, bias, which in ((2, "K", raw_k, bk, 0), (10, "Q", raw_q, bq, 1)):
                        if front and t == when:
                            u = Use(it, name)
                            act.wait_ge(work_ready, u.ready)
                            if it.at_least(0):
                                if which:
                                    act.wait_ge(qm_ready, it.lin(NH, NH))
                                else:
                                    act.wait_ge(kr_ready, it.lin(1, 1))
                            for k in range(KT):
                                a = nc.scalar.activation(raw[:, k, :], work[u.bank][:, k * S:(k + 1) * S],
                                                         ACT.Identity, bias=bias[:, k:k + 1])
                            a.then_inc(work_free[u.bank], 1)
                            act.wait_ge(work_free[u.bank], u.before + 1)
                            act.sem_inc(raw_ready, 1)
                    for when, name, there in ((6, "O", outs), (7, "Y", front)):
                        if there and t == when:
                            n = ln_before(it, name)
                            act.wait_ge(ln_chain, n * 2 + 2)
                            estimate_deviation(act, mv[:, :, 1], log[:], guess[:], log_chain, n, guess_ready)
                    if front and t == 9:
                        u = Use(it, "X")
                        act.wait_ge(work_ready, u.ready)
                        nc.scalar.copy(x1T[:].rearrange("p k s -> p (k s)"), work[u.bank][:]).then_inc(work_free[u.bank], 1)
                        act.wait_ge(work_free[u.bank], u.before + 1)
                        act.sem_inc(x1T_ready, 1)
                    if outs and t == 12:
                        u = Use(it, "OX")
                        act.wait_ge(work_ready, u.ready)
                        nc.scalar.copy(x2T[:].rearrange("p k s -> p (k s)"), work[u.bank][:]).then_inc(work_free[u.bank], 1)
                        act.wait_ge(work_free[u.bank], u.before + 1)
                        act.sem_inc(x2T_ready, 1)
                        act.wait_ge(x2_ready, it.lin(1, 0))
                        act.dma_start(dram["x2"][bass.ds(it.lin(S, -S), S), :].rearrange("(t p) d -> p t d", p=P),
                                      x2cur[:]).then_inc(x2_kept, 16)
                    if outs and t == 14:
                        u = Use(it, "R")
                        act.wait_ge(work_ready, u.ready)
                        nc.scalar.copy(r1[:, bass.ds(it.lin(S, -S), S)], work[u.bank][:, 0:S]).then_inc(work_free[u.bank], 1)

            for i in (-1, 0):
                step(Iter(0, i))
            with act.Fori(0, (NB - 2) // 2) as j:
                for r in (1, 2):
                    step(Iter(j, r))
            for i in (NB - 1, NB):
                step(Iter(0, i))
            act.wait_ge(x2_kept, 16 * NB)

        @block.vector
        def _(dve):
            dve.wait_ge(const_in, 16 * CONST_DMAS)
            dve.wait_ge(ones_set, 3)

            def met():
                dve.sem_inc(dve_met, 1)

            turn = [(d // DH) * DH + (d + DH // 2) % DH for d in range(32)]
            sums_from = [DH + d % DH for d in range(32)]

            def statistics(u, resid, n):
                dve.wait_ge(work_ready, u.ready)
                nc.vector.tensor_tensor(pre[:].rearrange("p t d -> p (t d)"), work[u.bank][:],
                                        resid[:].rearrange("p t d -> p (t d)"), ALU.add).then_inc(work_free[u.bank], 1)
                dve.wait_ge(work_free[u.bank], u.before + 1)
                for t in range(TT):
                    op = nc.vector.bn_stats(stats[:, t, :], pre[:, t, :])
                op.then_inc(ln_chain, 1)
                dve.wait_ge(ln_chain, n * 2 + 1)
                met()
                for t in range(TT):
                    op = nc.vector.bn_aggr(mv[:, t, :], stats[:, t, :])
                op.then_inc(ln_chain, 1)

            def normalise(out, done, n):
                dve.wait_ge(rstd_ready, n + 1)
                for t in range(TT):
                    op = nc.vector.tensor_scalar(out[:, t, :], pre[:, t, :], mv[:, t, 0:1], rstd[:, t:t + 1],
                                                 ALU.subtract, ALU.mult)
                op.then_inc(done, 1)

            def rotated(it, raw, which):
                dve.wait_ge(raw_ready, it.lin(2, 3 + which))
                if which:
                    dve.wait_ge(kr_ready, it.lin(1, 2))
                elif it.at_least(0):
                    dve.wait_ge(qr_ready, it.lin(1, 1))
                met()
                nc.vector.stream_shuffle(rot[:].rearrange("p k s -> p (k s)"), raw[:].rearrange("p k s -> p (k s)"),
                                         turn).then_inc(rot_chain, 1)
                dve.wait_ge(rot_chain, it.lin(2, 3 + which))
                nc.vector.tensor_tensor(rot[:], rot[:], sin[:].unsqueeze(1).to_broadcast([P, KT, S]),
                                        ALU.mult).then_inc(rot_ready, 1)

            def step(it):
                par = (it.r + 1) % 2
                front, outs = it.batch(1), it.batch(-1)
                for t in range(NH):
                    if it.batch(0):
                        dve.wait_ge(score_ready, it.lin(NH, t + 1))
                        if not (it.fixed and it.i == 0 and t < 2):
                            dve.wait_ge(probs_ready, it.lin(NH, t - 1))
                        met()
                        for q in range(TT):
                            op = nc.vector.tensor_tensor_reduce(
                                scored[t % 2][:, q, :], score[t % 2][:, q * S:(q + 1) * S], band[:, q, :],
                                -1.0 / DH ** 0.5, BIG, ALU.add, ALU.min, nmax[t % 2][:, q:q + 1])
                        op.then_inc(scored_ready, 1)
                    if t % 2 == 1 and (it.batch(0) if t >= 3 else it.batch(-1)):
                        dve.wait_ge(turned_ready, it.lin(NH, t - 2))
                        if not (it.fixed and it.i == 0 and t - 3 < NPT):
                            dve.wait_ge(attn_ready, it.lin(NG, (t - 3) // HG - 1))
                        nc.vector.tensor_copy(probsT[(t - 3) % NPT][:].rearrange("p t s -> p (t s)"),
                                              turned[0][:]).then_inc(probsT_even, 1)
                    if t % 4 == 0 and (it.batch(0) if t >= 8 else it.batch(-1)):
                        g = t // 4 - 2
                        bpar = (it.r if g >= 0 else it.r + 1) % 2
                        dve.wait_ge(attn_ready, it.lin(NG, g + 1))
                        if g == 0 and it.at_least(2):
                            dve.wait_ge(work_ready, Use(Iter(it.j, it.r - 1), "O").ready)
                        a = attn[g % 2][:, 0:S]
                        met()
                        nc.vector.stream_shuffle(sums[:], a, sums_from).then_inc(norm_chain, 1)
                        dve.wait_ge(norm_chain, it.lin(2 * NG, 2 * g + 1))
                        nc.vector.reciprocal(sums[:], sums[:]).then_inc(norm_chain, 1)
                        dve.wait_ge(norm_chain, it.lin(2 * NG, 2 * g + 2))
                        nc.vector.tensor_tensor(attnT[bpar][:, g % NG, :], a, sums[:], ALU.mult).then_inc(attnT_ready, 1)
                    if front and t == 1:
                        u = Use(it, "U")
                        dve.wait_ge(work_ready, u.ready)
                        for k in range(KT):
                            op = nc.vector.tensor_tensor_scan(state[:, k, :], acol[:, k:k + 1].to_broadcast([P, S]),
                                                              work[u.bank][:, k * S:(k + 1) * S], 0.0, ALU.mult, ALU.add)
                        op.then_inc(work_free[u.bank], 1)
                        dve.wait_ge(work_free[u.bank], u.before + 1)
                        dve.sem_inc(state_ready, 1)
                    if front and t == 3:
                        rotated(it, raw_k, 0)
                    if front and t == 4:
                        u = Use(it, "V")
                        dve.wait_ge(work_ready, u.ready)
                        if it.at_least(1):
                            dve.wait_ge(attn_ready, it.lin(NG, 0))
                        for k in range(TT):
                            op = nc.vector.tensor_tensor(vp[par][:, k, :, 0:DH],
                                                         work[u.bank][:, k * D:(k + 1) * D].rearrange("p (h d) -> p h d", d=DH),
                                                         bv[:].rearrange("p (h d) -> p h d", d=DH), ALU.add)
                        op.then_inc(work_free[u.bank], 1)
                        dve.wait_ge(work_free[u.bank], u.before + 1)
                        dve.sem_inc(vp_ready, 1)
                    if outs and t == 6:
                        dve.wait_ge(x1_ready, it.lin(1, 1) if it.batch(0) else NB)
                        statistics(Use(it, "O"), x1[(it.r + 1) % 2], ln_before(it, "O"))
                    if outs and t == 7:
                        if it.at_least(2):
                            dve.wait_ge(x2_kept, it.lin(16, -16))
                        normalise(x2cur, x2_ready, ln_before(it, "O"))
                    if front and t == 7:
                        dve.wait_ge(xb_ready, it.lin(1, 2))
                        if outs:
                            dve.wait_ge(x2_ready, it.lin(1, 0))
                        elif it.at_least(0):
                            dve.wait_ge(x1_ready, it.lin(1, 1))
                        statistics(Use(it, "Y"), xb, ln_before(it, "Y"))
                    if front and t == 8:
                        normalise(x1[par], x1_ready, ln_before(it, "Y"))
                    if front and t == 11:
                        rotated(it, raw_q, 1)

            for i in (-1, 0):
                step(Iter(0, i))
            with dve.Fori(0, (NB - 2) // 2) as j:
                for r in (1, 2):
                    step(Iter(j, r))
            for i in (NB - 1, NB):
                step(Iter(0, i))


def routing(nc, dram, keep):
    G = NB * NE // P
    GB = NB // G
    with ExitStack() as ctx:
        def sb(name, *shape, dt=F32):
            return ctx.enter_context(nc.sbuf_tensor(name, [P, *shape], dt))

        def sem(name):
            return ctx.enter_context(nc.semaphore(name))

        r1, ident = keep["r1"], keep["ident"]
        row_of, slot_of, weight_of = keep["row_of"], keep["slot_of"], keep["weight_of"]
        row_base, slot_base = sb("row_base", NC2), sb("slot_base", 1)
        rw2 = sb("rw2", NE)
        rw2_placed = sb("rw2_placed", GB, P)
        p = [sb(f"p{g}", S) for g in range(G)]
        nmax, total = sb("nmaxr", G), sb("total", G)
        top = [sb(f"top{g}", CAP) for g in range(G)]
        where = [sb(f"where{g}", CAP, dt=U32) for g in range(G)]
        token = [sb(f"token{g}", 2, CAP) for g in range(G)]
        weight = [sb(f"weight{g}", 2, CAP) for g in range(G)]
        wsum = sb("wsum", G)
        logits = [ctx.enter_context(nc.psum_tensor(f"logits{g}", [P, 512], F32)) for g in range(G)]
        turned = [ctx.enter_context(nc.psum_tensor(f"turnedr{n}", [P, 512], F32)) for n in range(2 * G)]

        rw2_in, zeroed, placed, silu_done = sem("rw2_in"), sem("zeroed"), sem("placed"), sem("silu_done")
        logits_ready, nmax_ready, exp_done = sem("logits_ready"), sem("nmax_ready"), sem("exp_done")
        chain, picked, rows_turned = sem("chain"), sem("picked"), sem("rows_turned")
        acc_set = sem("acc_set")
        block = ctx.enter_context(nc.Block())

        @block.sync
        def _(sp):
            sp.dma_start(rw2[:], dram["rw2"]).then_inc(rw2_in, 16)
            sp.dma_start(row_base[:], dram["row_base"]).then_inc(rw2_in, 16)
            sp.dma_start(slot_base[:], dram["slot_base"]).then_inc(rw2_in, 16)
            for c in range(NC2):
                sp.dma_start(dram["acc"][c], dram["x2"][c * 2 * S:(c + 1) * 2 * S, :]).then_inc(acc_set, 16)
            sp.wait_ge(acc_set, 16 * NC2)

        @block.gpsimd
        def _(pool):
            nc.gpsimd.memset(rw2_placed[:], 0.0).then_inc(zeroed, 1)
            pool.wait_ge(zeroed, 1)
            pool.wait_ge(rw2_in, 48)
            for c in range(GB):
                op = nc.gpsimd.tensor_copy(rw2_placed[:, c, c * NE:(c + 1) * NE], rw2[:])
            op.then_inc(placed, 1)

        @block.scalar
        def _(act):
            for g in range(G):
                half = r1[:, g * GB * S:(g + 1) * GB * S]
                nc.scalar.activation(half, half, ACT.Silu).then_inc(silu_done, 1)
            for g in range(G):
                act.wait_ge(nmax_ready, 1)
                nc.scalar.activation(p[g][:], logits[g][:, 0:S], ACT.Exp, bias=nmax[:, g:g + 1],
                                     accum_out=total[:, g:g + 1]).then_inc(exp_done, 1)

        @block.tensor
        def _(pe):
            pe.wait_ge(placed, 1)
            for g in range(G):
                pe.wait_ge(silu_done, g + 1)
                for c in range(GB):
                    b = g * GB + c
                    mm = nc.tensor.matmul(logits[g][:, 0:S], rw2_placed[:, c, :], r1[:, b * S:(b + 1) * S],
                                          start=(c == 0), stop=(c == GB - 1))
                mm.then_inc(logits_ready, 1)
            pe.wait_ge(picked, 1)
            for g in range(G):
                for n, src in enumerate((token, weight)):
                    nc.tensor.transpose(turned[2 * g + n][:, 0:P], src[g][:].rearrange("p a s -> p (a s)"),
                                        ident[:]).then_inc(rows_turned, 1)

        @block.vector
        def _(dve):
            links = [0]

            def link(op):
                links[0] += 1
                op.then_inc(chain, 1)
                dve.wait_ge(chain, links[0])

            dve.wait_ge(logits_ready, G)
            for g in range(G):
                op = nc.vector.tensor_reduce(nmax[:, g:g + 1], logits[g][:, 0:S], AX.X, ALU.max)
            link(op)
            nc.vector.tensor_scalar(nmax[:], nmax[:], -1.0, None, ALU.mult).then_inc(nmax_ready, 1)
            dve.wait_ge(exp_done, G)
            link(nc.vector.reciprocal(total[:], total[:]))
            for g in range(G):
                op = nc.vector.tensor_scalar(p[g][:], p[g][:], total[:, g:g + 1], None, ALU.mult)
            link(op)
            for r in range(CAP // 8):
                cols = slice(8 * r, 8 * r + 8)
                for g in range(G):
                    op = nc.vector.max(top[g][:, cols], p[g][:])
                link(op)
                for g in range(G):
                    nc.vector.max_index(where[g][:, cols], top[g][:, cols], p[g][:])
                    op = nc.vector.match_replace(p[g][:], top[g][:, cols], p[g][:], -1.0)
                link(op)
            for g in range(G):
                for a in range(2):
                    nc.vector.tensor_copy(token[g][:, a, :], where[g][:])
                op = nc.vector.tensor_reduce(wsum[:, g:g + 1], top[g][:], AX.X, ALU.add)
            link(op)
            link(nc.vector.tensor_scalar(wsum[:], wsum[:], 1e-9, None, ALU.add))
            link(nc.vector.reciprocal(wsum[:], wsum[:]))
            for g in range(G):
                for a in range(2):
                    op = nc.vector.tensor_scalar(weight[g][:, a, :], top[g][:], wsum[:, g:g + 1], None, ALU.mult)
            op.then_inc(picked, 1)
            for g in range(G):
                cs = slice(g * GB // 2, (g + 1) * GB // 2)
                dve.wait_ge(rows_turned, 2 * g + 2)
                dve.wait_ge(rw2_in, 48)
                for a in range(2):
                    half = slice(CAP * a, CAP * a + CAP)
                    tok, wgt = (turned[2 * g + n][half, 0:P].rearrange("p (c a e) -> p e c a", a=2, e=NE)[:, :, :, a]
                                for n in range(2))
                    base = row_base[half, cs].unsqueeze(1).to_broadcast([CAP, NE, GB // 2])
                    nc.vector.tensor_tensor(row_of[half, :, cs], tok, base, ALU.add)
                    nc.vector.tensor_scalar(slot_of[half, :, cs], tok, slot_base[half, 0:1], None, ALU.add)
                    op = nc.vector.tensor_copy(weight_of[half, :, cs], wgt)
            link(op)


def experts(nc, dram, keep):
    CB = NC2 // 2
    W = CB * P
    with ExitStack() as ctx:
        def sb(name, *shape, dt=F32):
            return ctx.enter_context(nc.sbuf_tensor(name, [P, *shape], dt))

        def ps(name):
            return ctx.enter_context(nc.psum_tensor(name, [P, 512], F32))

        def sem(name):
            return ctx.enter_context(nc.semaphore(name))

        ident, row_of, slot_of, weight_of = keep["ident"], keep["row_of"], keep["slot_of"], keep["weight_of"]
        SHAPES = ((KT, FF), (KT, FF), (FT, D))
        raw = [sb(f"raw{n}", *shape) for n, shape in enumerate(SHAPES)]
        w_hi = [[sb(f"w_hi{e}{n}", *shape, dt=F32R) for n, shape in enumerate(SHAPES)] for e in range(2)]
        w_lo = [[sb(f"w_lo{e}{n}", *shape, dt=F32R) for n, shape in enumerate(SHAPES)] for e in range(2)]
        rows_now = [sb(f"rows_now{n}", NC2, dt=U32) for n in range(2)]
        slots_now = [sb(f"slots_now{n}", NC2, dt=U32) for n in range(2)]
        rows = sb("rows", NC2, D)
        xT_hi = [sb(f"xT_hi{n}", KT, W, dt=F32R) for n in range(2)]
        xT_lo = [sb(f"xT_lo{n}", KT, W, dt=F32R) for n in range(2)]
        gate = [sb(f"gate{n}", W) for n in range(2)]
        hidden = [sb(f"hidden{n}", W) for n in range(2)]
        h_hi = [sb(f"h_hi{n}", FT, W, dt=F32R) for n in range(2)]
        h_lo = [sb(f"h_lo{n}", FT, W, dt=F32R) for n in range(2)]
        y = [sb(f"y{m}", D) for m in range(CB)]
        last = sb("last", 2, CB * 2 * TT, D)
        NT = CB * 2 * TT
        stats, mv, rstd = sb("stats3", 2, NT, 6), sb("mv3", 2, NT, 2), sb("rstd3", 2, NT)
        log, guess, newton = sb("log3", 2, NT), sb("guess3", 2, NT), sb("newton3", 2, NT)
        gate_bank = [ps(f"gate_bank{n}") for n in range(2)]
        value_bank = [ps(f"value_bank{n}") for n in range(2)]
        turn_bank = [ps(f"turn_bank{n}") for n in range(KT)]
        y_bank = [ps(f"y_bank{n}") for n in range(2)]

        raw_in, w_hi_ready, w_lo_ready = sem("raw_in"), sem("w_hi_ready"), sem("w_lo_ready")
        rows_taken, slots_taken, pool_met = sem("rows_taken"), sem("slots_taken"), sem("pool_met3")
        rows_in = [sem(f"rows_in{n}") for n in range(2)]
        rows_turned, xT_hi_ready, xT_lo_ready = sem("rows_turned3"), sem("xT_hi_ready"), sem("xT_lo_ready")
        product_ready, gate_ready, hidden_ready = sem("product_ready"), sem("gate_ready"), sem("hidden_ready")
        h_hi_ready, h_lo_ready = sem("h_hi_ready"), sem("h_lo_ready")
        y_ready, y_scaled = sem("y_ready"), sem("y_scaled")
        added = [sem(f"added{c}") for c in range(NC2)]
        last_in = [sem(f"last_in{n}") for n in range(2)]
        log_chain, guess_ready, newton_chain = sem("log_chain3"), sem("guess_ready3"), sem("newton_chain3")
        ln, rstd_ready, ln_done, out_done = sem("ln"), sem("rstd_ready3"), sem("ln_done"), sem("out_done")

        block = ctx.enter_context(nc.Block())

        def all_experts(eng, expert):
            for e in range(2):
                expert(Iter(0, e))
            with eng.Fori(1, NE // 2 - 1) as j:
                for r in range(2):
                    expert(Iter(j, r))
            for e in range(NE - 2, NE):
                expert(Iter(0, e))

        @block.sync
        def _(sp):
            def load(it):
                if it.at_least(1):
                    sp.wait_ge(w_lo_ready, it.lin(3, 0))
                for n, name in enumerate(("w1", "w2", "w3")):
                    src = dram[name][bass.ds(it.i, 1)].rearrange("o (k p) f -> p (o k) f", p=P)
                    sp.dma_start(raw[n][:], src).then_inc(raw_in, 16)

            all_experts(sp, load)
            for h in range(2):
                for m in range(CB):
                    c = CB * h + m
                    sp.wait_ge(added[c], 16 * NE)
                    sp.dma_start(last[:, h, m * 2 * TT:(m + 1) * 2 * TT, :],
                                 dram["acc"][c].rearrange("(t p) d -> p t d", p=P)).then_inc(last_in[h], 16)
            for h in range(2):
                sp.wait_ge(ln_done, h + 1)
                sp.dma_start(dram["out"][h * NB // 2:(h + 1) * NB // 2].rearrange("b (t p) d -> p (b t) d", p=P),
                             last[:, h, :, :]).then_inc(out_done, 16)
            sp.wait_ge(out_done, 32)

        @block.gpsimd
        def _(pool):
            def gather(it, h):
                par = it.r % 2
                if it.at_least(1):
                    pool.wait_ge(rows_turned, it.lin(2 * KT, (h - 1) * KT))
                    pool.sem_inc(pool_met, 1)
                for m in range(CB):
                    c = CB * h + m
                    nc.gpsimd.indirect_dma_start(
                        rows[:, c, :], None, dram["x2"],
                        bass.IndirectOffsetOnAxis(ap=rows_now[par][:, c:c + 1], axis=0)).then_inc(rows_in[h], 16)

            def take(it, now, source, taken):
                now = now[it.r % 2]
                nc.gpsimd.tensor_copy(now[:], source[:, bass.ds(it.i, 1), :].rearrange("p o c -> p (o c)")).then_inc(taken, 1)
                pool.wait_ge(taken, it.lin(1, 1))
                pool.sem_inc(pool_met, 1)

            def scatter(it, h):
                for m in range(CB):
                    c = CB * h + m
                    if it.at_least(1):
                        pool.wait_ge(added[c], it.lin(16, 0))
                    pool.wait_ge(y_scaled, it.lin(2 * CB, CB * h + m + 1))
                    pool.sem_inc(pool_met, 1)
                    nc.gpsimd.indirect_dma_start(
                        dram["acc"][c], bass.IndirectOffsetOnAxis(ap=slots_now[it.r % 2][:, c:c + 1], axis=0),
                        y[m][:], None, compute_op=ALU.add).then_inc(added[c], 16)

            def expert(it):
                more = not it.fixed or it.i < NE - 1
                nxt = Iter(it.j, it.r + 1)
                if more:
                    if it.at_least(1):
                        pool.wait_ge(rows_turned, it.lin(2 * KT, 0))
                    take(nxt, rows_now, row_of, rows_taken)
                    gather(nxt, 0)
                if it.at_least(1):
                    scatter(Iter(it.j, it.r - 1), 1)
                if more:
                    gather(nxt, 1)
                take(it, slots_now, slot_of, slots_taken)
                scatter(it, 0)

            take(Iter(0, 0), rows_now, row_of, rows_taken)
            for h in range(2):
                gather(Iter(0, 0), h)
            all_experts(pool, expert)
            scatter(Iter(0, NE - 1), 1)
            for h in range(2):
                pool.wait_ge(guess_ready, h + 1)
                refine_deviation(pool, lambda: None, mv[:, h, :, 1], guess[:, h, :], newton[:, h, :], rstd[:, h, :],
                                 newton_chain, 3 * h, rstd_ready)

        @block.tensor
        def _(pe):
            def product(out, pairs):
                n = 0
                for a, b in pairs:
                    for x, z in ((0, 0), (0, 1), (1, 0)):
                        n += 1
                        mm = nc.tensor.matmul(out, a[x], b[z], start=(n == 1), stop=(n == 3 * len(pairs)))
                return mm

            def turn(it, h):
                pe.wait_ge(rows_in[h], it.lin(16 * CB, 16 * CB))
                for k in range(KT):
                    if it.at_least(1) or h:
                        pe.wait_ge(xT_lo_ready, it.lin(2 * KT, (h - 1) * KT + k + 1))
                    for m in range(CB):
                        mm = nc.tensor.transpose(turn_bank[k][:, m * P:(m + 1) * P],
                                                 rows[:, CB * h + m, k * P:(k + 1) * P], ident[:])
                    mm.then_inc(rows_turned, 1)

            def up(it, h):
                par = it.r % 2
                pe.wait_ge(xT_lo_ready, it.lin(2 * KT, (h + 1) * KT))
                if h == 0:
                    pe.wait_ge(w_lo_ready, it.lin(3, 2))
                for f in range(FT):
                    if it.at_least(1) or h or f >= 2:
                        pe.wait_ge(gate_ready, it.lin(2 * FT, FT * h + f - 1))
                        pe.wait_ge(hidden_ready, it.lin(2 * FT, FT * h + f - 1))
                    cols = slice(f * P, (f + 1) * P)
                    for n, out in ((0, gate_bank[f % 2]), (1, value_bank[f % 2])):
                        mm = product(out[:], [((w_hi[par][n][:, k, cols], w_lo[par][n][:, k, cols]),
                                               (xT_hi[h][:, k, :], xT_lo[h][:, k, :])) for k in range(KT)])
                    mm.then_inc(product_ready, 1)

            def down(it, h):
                par = it.r % 2
                if h == 0:
                    pe.wait_ge(w_lo_ready, it.lin(3, 3))
                pe.wait_ge(h_lo_ready, it.lin(2 * FT, FT * (h + 1)))
                for m in range(CB):
                    if it.at_least(1) or h or m >= 2:
                        pe.wait_ge(y_scaled, it.lin(2 * CB, CB * h + m - 1))
                    cols = slice(m * P, (m + 1) * P)
                    mm = product(y_bank[m % 2][:, 0:D], [((h_hi[h][:, f, cols], h_lo[h][:, f, cols]),
                                                          (w_hi[par][2][:, f, :], w_lo[par][2][:, f, :])) for f in range(FT)])
                    mm.then_inc(y_ready, 1)

            def expert(it):
                up(it, 0)
                turn(it, 1)
                if it.at_least(1):
                    down(Iter(it.j, it.r - 1), 1)
                up(it, 1)
                if not it.fixed or it.i < NE - 1:
                    turn(Iter(it.j, it.r + 1), 0)
                down(it, 0)

            turn(Iter(0, 0), 0)
            all_experts(pe, expert)
            down(Iter(0, NE - 1), 1)

        @block.scalar
        def _(act):
            def split_weights(it):
                par = it.r % 2
                act.wait_ge(raw_in, it.lin(48, 48))
                if it.at_least(2):
                    act.wait_ge(y_ready, it.lin(2 * CB, -2 * CB))
                for n in range(3):
                    nc.scalar.copy(w_hi[par][n][:], raw[n][:]).then_inc(w_hi_ready, 1)

            def columns(it, h):
                if it.at_least(1):
                    act.wait_ge(product_ready, it.lin(2 * FT, FT * (h - 1)))
                for k in range(KT):
                    act.wait_ge(rows_turned, it.lin(2 * KT, h * KT + k + 1))
                    nc.scalar.copy(xT_hi[h][:, k, :], turn_bank[k][:]).then_inc(xT_hi_ready, 1)

            def h_high(it, h, f):
                act.wait_ge(hidden_ready, it.lin(2 * FT, FT * h + f + 1))
                if f == 0 and it.at_least(1):
                    act.wait_ge(y_ready, it.lin(2 * CB, CB * (h - 1)))
                nc.scalar.copy(h_hi[h][:, f, :], hidden[f % 2][:]).then_inc(h_hi_ready, 1)

            def weigh(it, h):
                for m in range(CB):
                    act.wait_ge(y_ready, it.lin(2 * CB, CB * h + m + 1))
                    if h:
                        act.wait_ge(added[m], it.lin(16, 16))
                    elif it.at_least(1):
                        act.wait_ge(added[CB + m], it.lin(16, 0))
                    nc.scalar.activation(y[m][:], y_bank[m % 2][:, 0:D], ACT.Copy,
                                         scale=weight_of[:, bass.ds(it.i, 1), CB * h + m]).then_inc(y_scaled, 1)

            def gates(it, h):
                for f in range(FT):
                    act.wait_ge(product_ready, it.lin(2 * FT, FT * h + f + 1))
                    if it.at_least(1) or h or f >= 2:
                        act.wait_ge(hidden_ready, it.lin(2 * FT, FT * h + f - 1))
                    nc.scalar.activation(gate[f % 2][:], gate_bank[f % 2][:], ACT.Silu).then_inc(gate_ready, 1)
                    if f:
                        h_high(it, h, f - 1)
                h_high(it, h, FT - 1)

            def expert(it):
                gates(it, 0)
                columns(it, 1)
                if it.at_least(1):
                    weigh(Iter(it.j, it.r - 1), 1)
                more = not it.fixed or it.i < NE - 1
                if more:
                    split_weights(Iter(it.j, it.r + 1))
                gates(it, 1)
                if more:
                    columns(Iter(it.j, it.r + 1), 0)
                weigh(it, 0)

            split_weights(Iter(0, 0))
            columns(Iter(0, 0), 0)
            act.preload_act_table(ACT.Silu)
            all_experts(act, expert)
            weigh(Iter(0, NE - 1), 1)
            act.preload_act_table_set("natural_log_exp_and_others")
            for h in range(2):
                act.wait_ge(ln, 2 * h + 2)
                estimate_deviation(act, mv[:, h, :, 1], log[:, h, :], guess[:, h, :], log_chain, h, guess_ready)

        @block.vector
        def _(dve):
            def split_weights(it):
                par = it.r % 2
                for n in range(3):
                    dve.wait_ge(w_hi_ready, it.lin(3, n + 1))
                    nc.vector.tensor_tensor(w_lo[par][n][:], raw[n][:], w_hi[par][n][:], ALU.subtract).then_inc(w_lo_ready, 1)

            def columns(it, h):
                for k in range(KT):
                    dve.wait_ge(xT_hi_ready, it.lin(2 * KT, h * KT + k + 1))
                    nc.vector.tensor_tensor(xT_lo[h][:, k, :], turn_bank[k][:], xT_hi[h][:, k, :],
                                            ALU.subtract).then_inc(xT_lo_ready, 1)

            def h_low(it, h, f):
                dve.wait_ge(h_hi_ready, it.lin(2 * FT, FT * h + f + 1))
                nc.vector.tensor_tensor(h_lo[h][:, f, :], hidden[f % 2][:], h_hi[h][:, f, :],
                                        ALU.subtract).then_inc(h_lo_ready, 1)

            def multiply(it, h):
                for f in range(FT):
                    dve.wait_ge(gate_ready, it.lin(2 * FT, FT * h + f + 1))
                    if it.at_least(1) or h or f >= 2:
                        dve.wait_ge(h_lo_ready, it.lin(2 * FT, FT * h + f - 1))
                    nc.vector.tensor_tensor(hidden[f % 2][:], gate[f % 2][:], value_bank[f % 2][:],
                                            ALU.mult).then_inc(hidden_ready, 1)
                    if f:
                        h_low(it, h, f - 1)
                h_low(it, h, FT - 1)

            def expert(it):
                multiply(it, 0)
                columns(it, 1)
                more = not it.fixed or it.i < NE - 1
                if more:
                    split_weights(Iter(it.j, it.r + 1))
                multiply(it, 1)
                if more:
                    columns(Iter(it.j, it.r + 1), 0)

            split_weights(Iter(0, 0))
            columns(Iter(0, 0), 0)
            all_experts(dve, expert)

            for h in range(2):
                dve.wait_ge(last_in[h], 16 * CB)
                for t in range(NT):
                    op = nc.vector.bn_stats(stats[:, h, t, :], last[:, h, t, :])
                op.then_inc(ln, 1)
                dve.wait_ge(ln, 2 * h + 1)
                for t in range(NT):
                    op = nc.vector.bn_aggr(mv[:, h, t, :], stats[:, h, t, :])
                op.then_inc(ln, 1)
            for h in range(2):
                dve.wait_ge(rstd_ready, h + 1)
                for t in range(NT):
                    op = nc.vector.tensor_scalar(last[:, h, t, :], last[:, h, t, :], mv[:, h, t, 0:1],
                                                 rstd[:, h, t:t + 1], ALU.subtract, ALU.mult)
                op.then_inc(ln_done, 1)


def program(nc, dram):
    with ExitStack() as ctx:
        def sb(name, *shape):
            return ctx.enter_context(nc.sbuf_tensor(name, [P, *shape], F32))

        keep = {"ident": sb("ident", P)}
        with nc.sbuf_tensor("r1", [P, NB * S], F32) as r1:
            keep["r1"] = r1
            mixing(nc, dram, keep)
            with ExitStack() as later:
                for name, dt in (("row_of", U32), ("slot_of", U32), ("weight_of", F32)):
                    keep[name] = later.enter_context(nc.sbuf_tensor(name, [P, NE, NC2], dt))
                routing(nc, dram, keep)
                experts(nc, dram, keep)


def kernel(**inputs):
    import numpy as np
    import concourse.bacc as bacc
    from concourse.bass_utils import run_bass_kernel_spmd

    a = {k: np.asarray(v) for k, v in inputs.items()}
    c = np.ascontiguousarray
    arrays = {
        "x": c(a["x"]), "xT": c(a["x"].transpose(0, 2, 1)), "cT": c(a["ctx_1024"].transpose(0, 2, 1)),
        "mix_A": c(a["L0_attn_A"].reshape(KT, P).T), "mix_BT": c(a["L0_attn_B"].T), "mix_WT": c(a["L0_attn_W"].T), "mix_b": c(a["L0_attn_b"]),
        "WqT": c(a["L0_xattn_Wq"].T), "bq": c(a["L0_xattn_bq"].reshape(KT, P).T), "WkT": c(a["L0_xattn_Wk"].T), "bk": c(a["L0_xattn_bk"].reshape(KT, P).T),
        "WvT": c(a["L0_xattn_Wv"].T), "bv": c(a["L0_xattn_bv"]), "WoT": c(a["L0_xattn_Wo"].T), "bo": c(a["L0_xattn_bo"]),
        "rw1": c(a["L0_ffn_router_w1"]), "rw2": c(a["L0_ffn_router_w2"]),
        "w1": c(a["L0_ffn_w1"]), "w2": c(a["L0_ffn_w2"]), "w3": c(a["L0_ffn_w3"]),
    }
    rows = np.arange(P)
    freq = (np.float32(1.0) / np.power(np.float32(10000.0), np.arange(0, DH, 2, dtype=np.float32) / np.float32(DH))).astype(np.float32)
    angle = (freq[rows % (DH // 2)][:, None] * np.arange(S, dtype=np.float32)[None, :]).astype(np.float32)
    sign = np.where(rows % DH < DH // 2, -1.0, 1.0)[:, None]
    pos = np.arange(S)
    arrays["cos"] = np.cos(angle.astype(np.float64)).astype(np.float32)
    arrays["sin"] = (sign * np.sin(angle.astype(np.float64))).astype(np.float32)
    arrays["band"] = np.where(np.abs(pos[:, None] - pos[None, :]) <= WINDOW, 0.0, MASKED).astype(np.float32)
    arrays["head_rows"] = (rows[:, None] // DH == np.arange(HPT)[None, :]).astype(np.float32)
    arrays["ident"] = np.eye(P, dtype=np.float32)
    arrays["slot_base"] = (S * (rows[:, None] // CAP)).astype(np.float32)
    arrays["row_base"] = (arrays["slot_base"] + 2 * S * np.arange(NC2)[None, :]).astype(np.float32)

    nc = bacc.Bacc("TRN2", target_bir_lowering=False, num_devices=1)
    dram = {k: nc.dram_tensor(f"in_{k}", v.shape, F32, kind="ExternalInput").ap() for k, v in arrays.items()}
    dram["x2"] = nc.dram_tensor("x2_rows", (NB * S, D), F32, kind="Internal").ap()
    dram["acc"] = [nc.dram_tensor(f"acc_rows{c}", (2 * S, D), F32, kind="Internal").ap() for c in range(NC2)]
    dram["out"] = nc.dram_tensor("out_0", (NB, S, D), F32, kind="ExternalOutput").ap()
    program(nc, dram)
    r = run_bass_kernel_spmd(nc, [{f"in_{k}": v for k, v in arrays.items()}], core_ids=[0])
    return r.results[0]["out_0"]
```

```python
from contextlib import ExitStack

import concourse.bass as bass
from concourse import mybir

F32 = mybir.dt.float32
F32R = mybir.dt.float32r
U32 = mybir.dt.uint32
ALU = mybir.AluOpType
ACT = mybir.ActivationFunctionType
AX = mybir.AxisListType

P = 128
NB = 16
S = 256
D = 256
KT = D // P
TT = S // P
NH = 16
DH = D // NH
HG = 4
NG = NH // HG
WINDOW = 50
SPAN = P + WINDOW
FIRST = P - WINDOW
TURN = 3
HID = 128
NE = 16
CAP = 64
FF = 512
FT = FF // P
NC2 = NB // 2
EPS = 1e-5
MASKED = -4e9
BIG = 3e38


class Iter:

    def __init__(self, j, r):
        self.j, self.r = j, r
        self.fixed = isinstance(j, int)
        self.i = 2 * j + r

    def lin(self, a, c):
        return self.j * (2 * a) + (a * self.r + c)

    def half(self, a, c):
        return self.j * a + (a * self.r + c) // 2

    def loads(self, d):
        return self.j * 48 + 48 * ((self.r + d) // 2 + 1)

    def batch(self, d):
        return not self.fixed or 0 <= self.i + d < NB

    def at_least(self, n):
        return not self.fixed or self.i >= n


FULL = ["U", "Y", "K", "X", "Q", "O", "V", "OX", "R"]
FRONT = [n for n in FULL if n not in ("O", "OX", "R")]
OUTS = ["O", "OX", "R"]
NF, NFR, NO = len(FULL), len(FRONT), len(OUTS)


class Use:

    def __init__(self, it, name):
        if it.fixed and it.i == -1:
            n = FRONT.index(name)
        elif it.fixed and it.i == 0:
            n = NFR + FRONT.index(name)
        elif it.fixed and it.i >= NB - 1:
            n = 2 * NFR + NF * (NB - 2) + NO * (it.i - NB + 1) + OUTS.index(name)
        else:
            c = 2 * NFR - NF + FULL.index(name)
            self.bank = (NF * it.r + c) % 2
            self.ready = it.lin(NF, c + 1)
            self.before = it.half(NF, c)
            self.first = False
            return
        self.bank, self.ready, self.before, self.first = n % 2, n + 1, n // 2, n < 2


def estimate_deviation(act, var, log, guess, chain, before, ready):
    act.activation(log, var, ACT.Ln, bias=EPS).then_inc(chain, 1)
    act.wait_ge(chain, before + 1)
    act.activation(guess, log, ACT.Exp, scale=-0.5).then_inc(ready, 1)


def refine_deviation(pool, met, var, guess, tmp, rstd, chain, before, ready):
    met()
    pool.tensor_scalar(rstd, var, EPS, None, ALU.add)
    pool.tensor_tensor(tmp, guess, guess, ALU.mult).then_inc(chain, 1)
    pool.wait_ge(chain, before + 1)
    pool.tensor_tensor(tmp, tmp, rstd, ALU.mult).then_inc(chain, 1)
    pool.wait_ge(chain, before + 2)
    met()
    pool.tensor_scalar(tmp, tmp, -0.5, 1.5, ALU.mult, ALU.add).then_inc(chain, 1)
    pool.wait_ge(chain, before + 3)
    pool.tensor_tensor(rstd, guess, tmp, ALU.mult).then_inc(ready, 1)


def ln_before(it, name):
    if it.fixed and it.i < 1:
        return it.i + 1
    if it.fixed and it.i >= NB - 1:
        return NB + it.i - 1
    return it.lin(2, 0 if name == "Y" else 1)


def mixing(nc, dram, keep):
    with ExitStack() as ctx:
        def sb(name, *shape, dt=F32):
            return ctx.enter_context(nc.sbuf_tensor(name, [P, *shape], dt))

        def ps(name):
            return ctx.enter_context(nc.psum_tensor(name, [P, 512], F32))

        def sem(name):
            return ctx.enter_context(nc.semaphore(name))

        r1 = keep["r1"]
        ident = keep["ident"]
        wb, ww = sb("wb", KT, D), sb("ww", KT, D)
        wq, wk, wv = sb("wq", KT, D), sb("wk", KT, D), sb("wv", KT, D)
        wo = sb("wo", NG, D)
        rw1 = sb("rw1", KT, HID)
        cos, sin = sb("cos", S), sb("sin", S)
        band = sb("band", TT, SPAN)
        acol, bq, bk = sb("acol", KT), sb("bq", KT), sb("bk", KT)
        b_mix, bv = sb("b_mix", D), sb("bv", D)
        xT = [sb(f"xT{n}", KT, S) for n in range(2)]
        cT = [sb(f"cT{n}", KT, S) for n in range(2)]
        xin = [sb(f"xin{n}", TT, D) for n in range(2)]
        state = sb("state", KT, S)
        xb, resid = sb("xb", TT, D), sb("resid", TT, D)
        pre = sb("pre", TT, D)
        stats, mv, rstd = sb("stats", TT, 6), sb("mv", TT, 2), sb("rstd", TT)
        log, guess, newton = sb("log", TT), sb("guess", TT), sb("newton", TT)
        x1 = [sb(f"x1_{n}", TT, D) for n in range(2)]
        x1T = sb("x1T", KT, S)
        raw = [sb("raw_k", KT, S), sb("raw_q", KT, S)]
        rot = sb("rot", KT, S)
        rope = sb("rope", KT, S)
        high, low = ([sb(f"{name}_{x}", KT, S, dt=F32R) for x in "kq"] for name in ("high", "low"))
        q_stack = [sb(f"q_stack{n}", 2, NH // 2, S, dt=F32R) for n in range(2)]
        k_stack = [sb(f"k_stack{n}", NH // 2, S, dt=F32R) for n in range(2)]
        vp = [sb(f"vp{n}", TT, NH, 2 * DH) for n in range(2)]
        NSB = 4
        scored = [sb(f"scored{n}", TT, SPAN) for n in range(NSB)]
        nmax = [sb(f"nmax{n}", TT) for n in range(NSB)]
        probs = [sb(f"probs{n}", TT, S) for n in range(NSB)]
        NPT = 8
        probsT = [sb(f"probsT{n}", TT, S) for n in range(NPT)]
        sums = [sb(f"sums{n}", S) for n in range(2)]
        sums_log = sb("sums_log", S)
        rough = [sb(f"rough{n}", S) for n in range(2)]
        inverse = [sb(f"inverse{n}", S) for n in range(2)]
        attnT = [sb(f"attnT{n}", NG, S) for n in range(2)]
        x2cur = sb("x2cur", TT, D)
        x2T = sb("x2T", KT, S)

        work = [ps(f"work{n}") for n in range(2)]
        score = [ps(f"score{n}") for n in range(2)]
        turned = [ps(f"turned{n}") for n in range(2)]
        attn = [ps(f"attn{n}") for n in range(2)]

        dve_met, pool_met, sp_met = sem("dve_met"), sem("pool_met"), sem("sp_met")
        const_in = sem("const_in")
        batch_in = [sem(f"batch_in{n}") for n in range(2)]
        fixed_set = sem("fixed_set")
        work_ready = sem("work_ready")
        work_free = [sem(f"work_free{n}") for n in range(2)]
        xb_ready, resid_ready = sem("xb_ready"), sem("resid_ready")
        state_ready = sem("state_ready")
        log_chain, guess_ready, newton_chain, rstd_ready = sem("log_chain"), sem("guess_ready"), sem("newton_chain"), sem("rstd_ready")
        ln_chain, rope_chain = sem("ln_chain"), sem("rope_chain")
        x1_ready, x1T_ready = sem("x1_ready"), sem("x1T_ready")
        raw_ready, rot_chain, rot_ready = sem("raw_ready"), sem("rot_chain"), sem("rot_ready")
        turned_done, high_ready = sem("turned_done"), sem("high_ready")
        parts_ready, parts_kept = sem("parts_ready"), sem("parts_kept")
        stacked = [sem("k_stacked"), sem("q_stacked")]
        vp_ready = sem("vp_ready")
        score_ready, scored_ready = sem("score_ready"), sem("scored_ready")
        probs_ready, turned_ready = sem("probs_ready"), sem("turned_ready")
        probsT_even, probsT_odd = sem("probsT_even"), sem("probsT_odd")
        attn_ready, attnT_ready = sem("attn_ready"), sem("attnT_ready")
        sums_ready, sums_log_ready, rough_ready = sem("sums_ready"), sem("sums_log_ready"), sem("rough_ready")
        inverse_chain, inverse_ready = sem("inverse_chain"), sem("inverse_ready")
        x2_ready, x2_kept, x2T_ready = sem("x2_ready"), sem("x2_kept"), sem("x2T_ready")

        consts = [
            (wb, dram["mix_BT"].rearrange("(k p) n -> p k n", p=P)),
            (ww, dram["mix_WT"].rearrange("(k p) n -> p k n", p=P)),
            (wq, dram["WqT"].rearrange("(k p) n -> p k n", p=P)),
            (wk, dram["WkT"].rearrange("(k p) n -> p k n", p=P)),
            (wv, dram["WvT"].rearrange("(k p) n -> p k n", p=P)),
            (rw1, dram["rw1"].rearrange("(k p) n -> p k n", p=P)),
            (cos, dram["cos"]), (sin, dram["sin"]),
            (band, dram["band"].rearrange("(t p) k -> p t k", p=P)),
            (ident, dram["ident"]),
            (acol, dram["mix_A"]),
            (bq, dram["bq"]),
            (bk, dram["bk"]),
            (b_mix, dram["mix_b"].partition_broadcast(P)),
            (bv, dram["bv"].partition_broadcast(P)),
        ]
        wo_rows = dram["WoT"].rearrange("(g q d) n -> q d g n", g=NG, q=HG)
        CONST_DMAS = len(consts) + HG + 1
        FIXED = 7 + NSB
        PARTS = ((0, 0, 1), (0, 1, 0))
        STACK_DMAS = 2 * 3

        block = ctx.enter_context(nc.Block())

        def there(it, t, lag):
            return it.batch(0) if t >= lag else it.batch(-1)

        def turn_number(it, which):
            return it.lin(2, 2 + which)

        @block.sync
        def _(sp):
            def load(par, b):
                sp.dma_start(xT[par][:], dram["xT"][b].rearrange("(k p) s -> p k s", p=P)).then_inc(batch_in[par], 16)
                sp.dma_start(cT[par][:], dram["cT"][b].rearrange("(k p) s -> p k s", p=P)).then_inc(batch_in[par], 16)
                sp.dma_start(xin[par][:], dram["x"][b].rearrange("(t p) d -> p t d", p=P)).then_inc(batch_in[par], 16)

            load(0, 0)
            for tile, src in consts:
                sp.dma_start(tile[:], src).then_inc(const_in, 16)
            sp.wait_ge(fixed_set, FIXED)
            for q in range(HG):
                sp.dma_start(wo[32 * q:32 * q + DH, :, :], wo_rows[q]).then_inc(const_in, 16)
            sp.dma_start(wo[DH:DH + 1, 0, :], dram["bo"].partition_broadcast(1)).then_inc(const_in, 16)
            load(1, 1)

            def met():
                sp.sem_inc(sp_met, 1)

            def stack(it, which):
                par = (it.r + 1) % 2
                sp.wait_ge(parts_ready, it.lin(2, 3 + which))
                met()
                if it.at_least(0):
                    sp.wait_ge(stacked[which], it.lin(16 * STACK_DMAS, 16 * STACK_DMAS))
                    met()
                for n, part in enumerate((high[which], low[which])):
                    sp.dma_start(dram["parts"][which, n], part[:].rearrange("p f s -> p (f s)").bitcast(F32)).then_inc(parts_kept, 16)
                sp.wait_ge(parts_kept, it.lin(64, 32 * (3 + which)))
                met()
                for c in range(3):
                    for a in range(2):
                        src = dram["parts"][which, PARTS[which][c], 64 * a:64 * a + 64].rearrange("(k d) s -> d k s", d=DH)
                        rows = slice(64 * a + DH * c, 64 * a + DH * c + DH)
                        dst = q_stack[par][rows, a] if which else k_stack[par][rows]
                        sp.dma_start(dst.rearrange("d (k f) s -> d k (f s)", f=KT).bitcast(F32), src).then_inc(stacked[which], 16)

            def step(it, more):
                later = it.lin(1, 3)
                if it.at_least(1):
                    sp.wait_ge(score_ready, it.lin(NH, 0))
                    met()
                stack(it, 0)
                stack(it, 1)
                if more:
                    sp.wait_ge(work_ready, Use(it, "V").ready)
                    met()
                    sp.wait_ge(xb_ready, it.lin(1, 2))
                    met()
                    load((it.r + 1) % 2, later)

            for i in (-1, 0):
                step(Iter(0, i), True)
            with sp.Fori(0, (NB - 4) // 2) as j:
                for r in (1, 2):
                    step(Iter(j, r), True)
            for r in (1, 2):
                step(Iter((NB - 4) // 2, r), False)

        @block.gpsimd
        def _(pool):
            nc.gpsimd.memset(wo[:], 0.0).then_inc(fixed_set, 1)
            for n in range(2):
                nc.gpsimd.memset(k_stack[n][:].bitcast(F32), 0.0).then_inc(fixed_set, 1)
                nc.gpsimd.memset(q_stack[n][:].bitcast(F32), 0.0).then_inc(fixed_set, 1)
            pool.wait_ge(const_in, 16 * CONST_DMAS)

            def met():
                pool.sem_inc(pool_met, 1)

            def rotate(it, which):
                n = turn_number(it, which)
                pool.wait_ge(raw_ready, n + 1)
                nc.gpsimd.tensor_tensor(rope[:], raw[which][:], cos[:].unsqueeze(1).to_broadcast([P, KT, S]),
                                        ALU.mult).then_inc(rope_chain, 1)
                pool.wait_ge(rope_chain, n + 1)
                pool.wait_ge(rot_ready, n + 1)
                nc.gpsimd.tensor_tensor(raw[which][:], rope[:], rot[:], ALU.add).then_inc(turned_done, 1)
                pool.wait_ge(high_ready, n + 1)
                nc.gpsimd.tensor_tensor(low[which][:], raw[which][:], high[which][:].bitcast(F32),
                                        ALU.subtract).then_inc(parts_ready, 1)

            def inverse_deviation(n):
                pool.wait_ge(guess_ready, n + 1)
                refine_deviation(pool, met, mv[:, :, 1], guess[:], newton[:], rstd[:], newton_chain, n * 3, rstd_ready)

            def inverse_sums(it, g):
                b = g % 2
                pool.wait_ge(rough_ready, it.lin(NG, g + 1))
                nc.gpsimd.tensor_tensor(inverse[b][:], sums[b][:], rough[b][:], ALU.mult).then_inc(inverse_chain, 1)
                pool.wait_ge(inverse_chain, it.lin(2 * NG, 2 * g + 1))
                met()
                nc.gpsimd.tensor_scalar(inverse[b][:], inverse[b][:], -1.0, 2.0, ALU.mult, ALU.add).then_inc(inverse_chain, 1)
                pool.wait_ge(inverse_chain, it.lin(2 * NG, 2 * g + 2))
                nc.gpsimd.tensor_tensor(inverse[b][:], inverse[b][:], rough[b][:], ALU.mult).then_inc(inverse_ready, 1)

            def step(it):
                par = (it.r + 1) % 2
                front, outs = it.batch(1), it.batch(-1)
                if front:
                    pool.wait_ge(batch_in[par], it.loads(1))
                    if it.at_least(0):
                        pool.wait_ge(x1_ready, it.lin(1, 1))
                    nc.gpsimd.tensor_tensor(xb[:], xin[par][:], b_mix[:].unsqueeze(1).to_broadcast([P, TT, D]),
                                            ALU.add).then_inc(xb_ready, 1)
                if outs:
                    pool.wait_ge(x1_ready, it.lin(1, 0))
                    if it.at_least(2):
                        pool.wait_ge(x2_ready, it.lin(1, 0))
                    met()
                    nc.gpsimd.tensor_copy(resid[:], x1[par][:]).then_inc(resid_ready, 1)
                    inverse_sums(it, -2)
                if front:
                    inverse_deviation(ln_before(it, "Y"))
                if outs:
                    inverse_sums(it, -1)
                if front:
                    rotate(it, 0)
                    rotate(it, 1)
                if it.batch(0):
                    inverse_sums(it, 0)
                if outs:
                    inverse_deviation(ln_before(it, "O"))
                if it.batch(0):
                    inverse_sums(it, 1)

            for i in (-1, 0):
                step(Iter(0, i))
            with pool.Fori(0, (NB - 2) // 2) as j:
                for r in (1, 2):
                    step(Iter(j, r))
            for i in (NB - 1, NB):
                step(Iter(0, i))

        @block.tensor
        def _(pe):
            pe.wait_ge(const_in, 16 * CONST_DMAS)
            pe.wait_ge(fixed_set, FIXED)

            def begin(u):
                if not u.first:
                    pe.wait_ge(work_free[u.bank], u.before)
                return work[u.bank]

            def heads(it, t):
                if it.batch(0):
                    if not (it.fixed and it.i == 0 and t < 2):
                        pe.wait_ge(scored_ready, it.lin(NH, t - 1))
                    if t == 0:
                        for s in stacked:
                            pe.wait_ge(s, it.lin(16 * STACK_DMAS, 16 * STACK_DMAS))
                    for q in range(TT):
                        mm = nc.tensor.matmul(score[t % 2][:, q * SPAN:(q + 1) * SPAN],
                                              q_stack[it.r % 2][:, t % 2, t // 2, q * P:(q + 1) * P],
                                              k_stack[it.r % 2][:, t // 2, q * FIRST:q * FIRST + SPAN], start=True, stop=True)
                    mm.then_inc(score_ready, 1)
                if there(it, t, TURN):
                    h = t - TURN
                    pe.wait_ge(probs_ready, it.lin(NH, h + 1))
                    if not (it.fixed and it.i == 0 and h < 2):
                        pe.wait_ge(probsT_odd if h % 2 else probsT_even, it.half(NH, h))
                    for q in range(TT):
                        for k in range(TT):
                            mm = nc.tensor.transpose(turned[h % 2][:, k * S + q * P:k * S + (q + 1) * P],
                                                     probs[h % NSB][:, q, k * P:(k + 1) * P], ident[:])
                    mm.then_inc(turned_ready, 1)
                if t % 4 == 0 and there(it, t, 8):
                    g = (t - 8) // 4
                    vpar = (it.r if g >= 0 else it.r + 1) % 2
                    pe.wait_ge(probsT_even, it.lin(2 * NG, 2 * (g + 1)))
                    pe.wait_ge(probsT_odd, it.lin(2 * NG, 2 * (g + 1)))
                    pe.wait_ge(vp_ready, it.lin(1, 1 if g >= 0 else 0))
                    if not (it.fixed and it.i == 0 and g < 2):
                        pe.wait_ge(attnT_ready, it.lin(NG, g - 1))
                    for k in range(TT):
                        for q in range(HG):
                            h = HG * (g % NG) + q
                            mm = nc.tensor.matmul(attn[g % 2][32 * q:32 * q + 32, 0:S], vp[vpar][:, k, h, :],
                                                  probsT[(HG * g + q) % NPT][:, k, :],
                                                  start=(k == 0), stop=(k == TT - 1))
                    mm.then_inc(attn_ready, 1)

            def step(it):
                par = (it.r + 1) % 2
                front, outs = it.batch(1), it.batch(-1)
                for t in range(NH):
                    heads(it, t)
                    if front and t == 0:
                        u = Use(it, "U")
                        pe.wait_ge(batch_in[par], it.loads(1))
                        w = begin(u)
                        for n in range(KT):
                            for k in range(KT):
                                mm = nc.tensor.matmul(w[:, n * S:(n + 1) * S], wb[:, k, n * P:(n + 1) * P],
                                                      xT[par][:, k, :], start=(k == 0), stop=(k == KT - 1))
                        mm.then_inc(work_ready, 1)
                    if front and t == 2:
                        w = begin(Use(it, "Y"))
                        pe.wait_ge(state_ready, it.lin(1, 2))
                        for n in range(TT):
                            for k in range(KT):
                                mm = nc.tensor.matmul(w[:, n * D:(n + 1) * D], state[:, k, n * P:(n + 1) * P],
                                                      ww[:, k, :], start=(k == 0), stop=(k == KT - 1))
                        mm.then_inc(work_ready, 1)
                    if front and t == 3:
                        w = begin(Use(it, "K"))
                        for n in range(KT):
                            for k in range(KT):
                                mm = nc.tensor.matmul(w[:, n * S:(n + 1) * S], wk[:, k, n * P:(n + 1) * P],
                                                      cT[par][:, k, :], start=(k == 0), stop=(k == KT - 1))
                        mm.then_inc(work_ready, 1)
                    if front and t == 6:
                        w = begin(Use(it, "X"))
                        pe.wait_ge(x1_ready, it.lin(1, 2))
                        for k in range(KT):
                            for n in range(TT):
                                mm = nc.tensor.transpose(w[:, k * S + n * P:k * S + (n + 1) * P],
                                                         x1[par][:, n, k * P:(k + 1) * P], ident[:])
                        mm.then_inc(work_ready, 1)
                    if front and t == 7:
                        w = begin(Use(it, "Q"))
                        pe.wait_ge(x1T_ready, it.lin(1, 2))
                        for n in range(KT):
                            for k in range(KT):
                                mm = nc.tensor.matmul(w[:, n * S:(n + 1) * S], wq[:, k, n * P:(n + 1) * P],
                                                      x1T[:, k, :], start=(k == 0), stop=(k == KT - 1))
                        mm.then_inc(work_ready, 1)
                    if outs and t in (8, 9):
                        n = t - 8
                        if n == 0:
                            w = begin(Use(it, "O"))
                            pe.wait_ge(attnT_ready, it.lin(NG, 0))
                        for g in range(NG):
                            mm = nc.tensor.matmul(w[:, n * D:(n + 1) * D], attnT[(it.r + 1) % 2][:, g, n * P:(n + 1) * P],
                                                  wo[:, g, :], start=(g == 0), stop=(g == NG - 1))
                        if n == TT - 1:
                            mm.then_inc(work_ready, 1)
                    if front and t == 11:
                        w = begin(Use(it, "V"))
                        for n in range(TT):
                            for k in range(KT):
                                mm = nc.tensor.matmul(w[:, n * D:(n + 1) * D], cT[par][:, k, n * P:(n + 1) * P],
                                                      wv[:, k, :], start=(k == 0), stop=(k == KT - 1))
                        mm.then_inc(work_ready, 1)
                    if outs and t == 13:
                        w = begin(Use(it, "OX"))
                        pe.wait_ge(x2_ready, it.lin(1, 1))
                        for k in range(KT):
                            for n in range(TT):
                                mm = nc.tensor.transpose(w[:, k * S + n * P:k * S + (n + 1) * P],
                                                         x2cur[:, n, k * P:(k + 1) * P], ident[:])
                        mm.then_inc(work_ready, 1)
                    if outs and t == 15:
                        w = begin(Use(it, "R"))
                        pe.wait_ge(x2T_ready, it.lin(1, 0))
                        for k in range(KT):
                            mm = nc.tensor.matmul(w[:, 0:S], rw1[:, k, :], x2T[:, k, :],
                                                  start=(k == 0), stop=(k == KT - 1))
                        mm.then_inc(work_ready, 1)

            for i in (-1, 0):
                step(Iter(0, i))
            with pe.Fori(0, (NB - 2) // 2) as j:
                for r in (1, 2):
                    step(Iter(j, r))
            for i in (NB - 1, NB):
                step(Iter(0, i))

        @block.scalar
        def _(act):
            act.wait_ge(const_in, 16 * CONST_DMAS)
            act.wait_ge(fixed_set, FIXED)
            act.sem_inc(x2_kept, 1)
            act.sem_inc(x2_ready, 1)
            act.preload_act_table_set("natural_log_exp_and_others")

            def step(it):
                front, outs = it.batch(1), it.batch(-1)
                for t in range(NH):
                    for when, name, here in ((4, "Y", front), (11, "O", outs)):
                        if here and t == when:
                            n = ln_before(it, name)
                            act.wait_ge(ln_chain, n * 2 + 2)
                            estimate_deviation(act, mv[:, :, 1], log[:], guess[:], log_chain, n, guess_ready)
                    h = t - TURN - 1
                    if h % 2 == 1 and there(it, t, TURN + 1):
                        act.wait_ge(turned_ready, it.lin(NH, h + 1))
                        if not (it.fixed and it.i == 0 and h < NPT):
                            act.wait_ge(attn_ready, it.lin(NG, h // HG - 1))
                        nc.scalar.copy(probsT[h % NPT][:].rearrange("p t s -> p (t s)"),
                                       turned[1][:]).then_inc(probsT_odd, 1)
                    for when, which in ((8, 0), (10, 1)):
                        if front and t == when:
                            n = turn_number(it, which)
                            act.wait_ge(turned_done, n + 1)
                            if it.at_least(0):
                                act.wait_ge(parts_kept, it.lin(64, 32 * (1 + which)))
                            nc.scalar.copy(high[which][:], raw[which][:]).then_inc(high_ready, 1)
                    if outs and t == 14:
                        u = Use(it, "OX")
                        act.wait_ge(work_ready, u.ready)
                        nc.scalar.copy(x2T[:].rearrange("p k s -> p (k s)"), work[u.bank][:]).then_inc(work_free[u.bank], 1)
                        act.wait_ge(work_free[u.bank], u.before + 1)
                        act.sem_inc(x2T_ready, 1)
                        act.wait_ge(x2_ready, it.lin(1, 1))
                        act.dma_start(dram["x2"][bass.ds(it.lin(S, -S), S), :].rearrange("(t p) d -> p t d", p=P),
                                      x2cur[:]).then_inc(x2_kept, 16)
                    if t % 4 == 1 and there(it, t, 9):
                        g = (t - 9) // 4
                        act.wait_ge(sums_ready, it.lin(NG, g + 1))
                        nc.scalar.activation(sums_log[:], sums[g % 2][:], ACT.Ln).then_inc(sums_log_ready, 1)
                        act.wait_ge(sums_log_ready, it.lin(NG, g + 1))
                        nc.scalar.activation(rough[g % 2][:], sums_log[:], ACT.Exp, scale=-1.0).then_inc(rough_ready, 1)
                    if it.batch(0):
                        act.wait_ge(scored_ready, it.lin(NH, t + 1))
                        if not (it.fixed and it.i == 0 and t < NSB):
                            act.wait_ge(turned_ready, it.lin(NH, t + 1 - NSB))
                        for q in range(TT):
                            a = nc.scalar.activation(probs[t % NSB][:, q, q * FIRST:q * FIRST + SPAN], scored[t % NSB][:, q, :],
                                                     ACT.Exp, bias=nmax[t % NSB][:, q:q + 1], scale=-1.0)
                        a.then_inc(probs_ready, 1)
                    for when, name, bias, which in ((4, "K", bk, 0), (8, "Q", bq, 1)):
                        if front and t == when:
                            u = Use(it, name)
                            act.wait_ge(work_ready, u.ready)
                            if it.at_least(0):
                                act.wait_ge(parts_ready, turn_number(it, which) - 1)
                            for k in range(KT):
                                a = nc.scalar.activation(raw[which][:, k, :], work[u.bank][:, k * S:(k + 1) * S],
                                                         ACT.Identity, bias=bias[:, k:k + 1])
                            a.then_inc(work_free[u.bank], 1)
                            act.wait_ge(work_free[u.bank], u.before + 1)
                            act.sem_inc(raw_ready, 1)
                    if outs and t == 15:
                        u = Use(it, "R")
                        act.wait_ge(work_ready, u.ready)
                        nc.scalar.copy(r1[:, bass.ds(it.lin(S, -S), S)], work[u.bank][:, 0:S]).then_inc(work_free[u.bank], 1)
                    if front and t == 6:
                        u = Use(it, "X")
                        act.wait_ge(work_ready, u.ready)
                        nc.scalar.copy(x1T[:].rearrange("p k s -> p (k s)"), work[u.bank][:]).then_inc(work_free[u.bank], 1)
                        act.wait_ge(work_free[u.bank], u.before + 1)
                        act.sem_inc(x1T_ready, 1)

            for i in (-1, 0):
                step(Iter(0, i))
            with act.Fori(0, (NB - 2) // 2) as j:
                for r in (1, 2):
                    step(Iter(j, r))
            for i in (NB - 1, NB):
                step(Iter(0, i))
            act.wait_ge(x2_kept, 16 * NB + 1)

        @block.vector
        def _(dve):
            for n in range(2):
                nc.vector.memset(vp[n][:], 1.0).then_inc(fixed_set, 1)
            for n in range(NSB):
                nc.vector.memset(probs[n][:], 0.0).then_inc(fixed_set, 1)
            dve.wait_ge(const_in, 16 * CONST_DMAS)
            dve.wait_ge(fixed_set, FIXED)

            def met():
                dve.sem_inc(dve_met, 1)

            turn = [(d // DH) * DH + (d + DH // 2) % DH for d in range(32)]
            sums_from = [DH + d % DH for d in range(32)]

            def statistics(u, added, n):
                dve.wait_ge(work_ready, u.ready)
                nc.vector.tensor_tensor(pre[:].rearrange("p t d -> p (t d)"), work[u.bank][:],
                                        added[:].rearrange("p t d -> p (t d)"), ALU.add).then_inc(work_free[u.bank], 1)
                dve.wait_ge(work_free[u.bank], u.before + 1)
                for t in range(TT):
                    op = nc.vector.bn_stats(stats[:, t, :], pre[:, t, :])
                op.then_inc(ln_chain, 1)
                dve.wait_ge(ln_chain, n * 2 + 1)
                met()
                for t in range(TT):
                    op = nc.vector.bn_aggr(mv[:, t, :], stats[:, t, :])
                op.then_inc(ln_chain, 1)

            def normalise(out, done, n):
                dve.wait_ge(rstd_ready, n + 1)
                for t in range(TT):
                    op = nc.vector.tensor_scalar(out[:, t, :], pre[:, t, :], mv[:, t, 0:1], rstd[:, t:t + 1],
                                                 ALU.subtract, ALU.mult)
                op.then_inc(done, 1)

            def rotated(it, which):
                n = turn_number(it, which)
                dve.wait_ge(raw_ready, n + 1)
                if which or it.at_least(0):
                    dve.wait_ge(turned_done, n)
                met()
                nc.vector.stream_shuffle(rot[:].rearrange("p k s -> p (k s)"), raw[which][:].rearrange("p k s -> p (k s)"),
                                         turn).then_inc(rot_chain, 1)
                dve.wait_ge(rot_chain, n + 1)
                nc.vector.tensor_tensor(rot[:], rot[:], sin[:].unsqueeze(1).to_broadcast([P, KT, S]),
                                        ALU.mult).then_inc(rot_ready, 1)

            def step(it):
                par = (it.r + 1) % 2
                front, outs = it.batch(1), it.batch(-1)
                for t in range(NH):
                    h = t - TURN - 1
                    if h % 2 == 0 and there(it, t, TURN + 1):
                        dve.wait_ge(turned_ready, it.lin(NH, h + 1))
                        if not (it.fixed and it.i == 0 and h < NPT):
                            dve.wait_ge(attn_ready, it.lin(NG, h // HG - 1))
                        nc.vector.tensor_copy(probsT[h % NPT][:].rearrange("p t s -> p (t s)"),
                                              turned[0][:]).then_inc(probsT_even, 1)
                    if front and t == 9:
                        rotated(it, 1)
                    if t % 4 == 1 and there(it, t, 9):
                        g = (t - 9) // 4
                        dve.wait_ge(attn_ready, it.lin(NG, g + 1))
                        met()
                        nc.vector.stream_shuffle(sums[g % 2][:], attn[g % 2][:, 0:S], sums_from).then_inc(sums_ready, 1)
                    if it.batch(0):
                        dve.wait_ge(score_ready, it.lin(NH, t + 1))
                        if not (it.fixed and it.i == 0 and t < NSB):
                            dve.wait_ge(probs_ready, it.lin(NH, t + 1 - NSB))
                        met()
                        for q in range(TT):
                            op = nc.vector.tensor_tensor_reduce(
                                scored[t % NSB][:, q, :], score[t % 2][:, q * SPAN:(q + 1) * SPAN], band[:, q, :],
                                -1.0 / DH ** 0.5, BIG, ALU.add, ALU.min, nmax[t % NSB][:, q:q + 1])
                        op.then_inc(scored_ready, 1)
                    if t % 4 == 3 and there(it, t, 11):
                        g = (t - 11) // 4
                        bpar = (it.r if g >= 0 else it.r + 1) % 2
                        dve.wait_ge(inverse_ready, it.lin(NG, g + 1))
                        if g == 0 and it.at_least(2):
                            dve.wait_ge(work_ready, Use(Iter(it.j, it.r - 1), "O").ready)
                        nc.vector.tensor_tensor(attnT[bpar][:, g % NG, :], attn[g % 2][:, 0:S], inverse[g % 2][:],
                                                ALU.mult).then_inc(attnT_ready, 1)
                    if front and t == 1:
                        u = Use(it, "U")
                        dve.wait_ge(work_ready, u.ready)
                        for k in range(KT):
                            op = nc.vector.tensor_tensor_scan(state[:, k, :], acol[:, k:k + 1].to_broadcast([P, S]),
                                                              work[u.bank][:, k * S:(k + 1) * S], 0.0, ALU.mult, ALU.add)
                        op.then_inc(work_free[u.bank], 1)
                        dve.wait_ge(work_free[u.bank], u.before + 1)
                        dve.sem_inc(state_ready, 1)
                    if front and t == 3:
                        dve.wait_ge(xb_ready, it.lin(1, 2))
                        if it.at_least(2):
                            dve.wait_ge(x2_ready, it.lin(1, 0))
                        elif it.at_least(0):
                            dve.wait_ge(x1_ready, it.lin(1, 1))
                        statistics(Use(it, "Y"), xb, ln_before(it, "Y"))
                    if front and t == 5:
                        if outs:
                            dve.wait_ge(resid_ready, it.lin(1, 0))
                        normalise(x1[par], x1_ready, ln_before(it, "Y"))
                    if outs and t == 12:
                        if it.at_least(2):
                            dve.wait_ge(x2_kept, it.lin(16, -15))
                        normalise(x2cur, x2_ready, ln_before(it, "O"))
                    if front and t == 12:
                        u = Use(it, "V")
                        dve.wait_ge(work_ready, u.ready)
                        if it.at_least(1):
                            dve.wait_ge(attn_ready, it.lin(NG, 0))
                        for k in range(TT):
                            op = nc.vector.tensor_tensor(vp[par][:, k, :, 0:DH],
                                                         work[u.bank][:, k * D:(k + 1) * D].rearrange("p (h d) -> p h d", d=DH),
                                                         bv[:].rearrange("p (h d) -> p h d", d=DH), ALU.add)
                        op.then_inc(work_free[u.bank], 1)
                        dve.wait_ge(work_free[u.bank], u.before + 1)
                        dve.sem_inc(vp_ready, 1)
                    if front and t == 6:
                        rotated(it, 0)
                    if outs and t == 10:
                        dve.wait_ge(resid_ready, it.lin(1, 0))
                        dve.wait_ge(x1_ready, it.lin(1, 2) if front else NB)
                        if not front:
                            dve.wait_ge(x2_ready, it.lin(1, 0))
                        statistics(Use(it, "O"), resid, ln_before(it, "O"))

            for i in (-1, 0):
                step(Iter(0, i))
            with dve.Fori(0, (NB - 2) // 2) as j:
                for r in (1, 2):
                    step(Iter(j, r))
            for i in (NB - 1, NB):
                step(Iter(0, i))


def routing(nc, dram, keep):
    G = NB * NE // P
    GB = NB // G
    with ExitStack() as ctx:
        def sb(name, *shape, dt=F32):
            return ctx.enter_context(nc.sbuf_tensor(name, [P, *shape], dt))

        def sem(name):
            return ctx.enter_context(nc.semaphore(name))

        r1, ident = keep["r1"], keep["ident"]
        row_of, slot_of, weight_of = keep["row_of"], keep["slot_of"], keep["weight_of"]
        row_base, slot_base = sb("row_base", NC2), sb("slot_base", 1)
        rw2 = sb("rw2", NE)
        rw2_placed = sb("rw2_placed", GB, P)
        p = [sb(f"p{g}", S) for g in range(G)]
        nmax, total = sb("nmaxr", G), sb("total", G)
        top = [sb(f"top{g}", CAP) for g in range(G)]
        where = [sb(f"where{g}", CAP, dt=U32) for g in range(G)]
        token = [sb(f"token{g}", 2, CAP) for g in range(G)]
        weight = [sb(f"weight{g}", 2, CAP) for g in range(G)]
        wsum = sb("wsum", G)
        logits = [ctx.enter_context(nc.psum_tensor(f"logits{g}", [P, 512], F32)) for g in range(G)]
        turned = [ctx.enter_context(nc.psum_tensor(f"turnedr{n}", [P, 512], F32)) for n in range(2 * G)]

        rw2_in, zeroed, placed, silu_done = sem("rw2_in"), sem("zeroed"), sem("placed"), sem("silu_done")
        logits_ready, nmax_ready, exp_done = sem("logits_ready"), sem("nmax_ready"), sem("exp_done")
        chain, picked, rows_turned = sem("chain"), sem("picked"), sem("rows_turned")
        acc_set = sem("acc_set")
        block = ctx.enter_context(nc.Block())

        @block.sync
        def _(sp):
            sp.dma_start(rw2[:], dram["rw2"]).then_inc(rw2_in, 16)
            sp.dma_start(row_base[:], dram["row_base"]).then_inc(rw2_in, 16)
            sp.dma_start(slot_base[:], dram["slot_base"]).then_inc(rw2_in, 16)
            for c in range(NC2):
                sp.dma_start(dram["acc"][c], dram["x2"][c * 2 * S:(c + 1) * 2 * S, :]).then_inc(acc_set, 16)
            sp.wait_ge(acc_set, 16 * NC2)

        @block.gpsimd
        def _(pool):
            nc.gpsimd.memset(rw2_placed[:], 0.0).then_inc(zeroed, 1)
            pool.wait_ge(zeroed, 1)
            pool.wait_ge(rw2_in, 48)
            for c in range(GB):
                op = nc.gpsimd.tensor_copy(rw2_placed[:, c, c * NE:(c + 1) * NE], rw2[:])
            op.then_inc(placed, 1)

        @block.scalar
        def _(act):
            for g in range(G):
                half = r1[:, g * GB * S:(g + 1) * GB * S]
                nc.scalar.activation(half, half, ACT.Silu).then_inc(silu_done, 1)
            for g in range(G):
                act.wait_ge(nmax_ready, 1)
                nc.scalar.activation(p[g][:], logits[g][:, 0:S], ACT.Exp, bias=nmax[:, g:g + 1],
                                     accum_out=total[:, g:g + 1]).then_inc(exp_done, 1)

        @block.tensor
        def _(pe):
            pe.wait_ge(placed, 1)
            for g in range(G):
                pe.wait_ge(silu_done, g + 1)
                for c in range(GB):
                    b = g * GB + c
                    mm = nc.tensor.matmul(logits[g][:, 0:S], rw2_placed[:, c, :], r1[:, b * S:(b + 1) * S],
                                          start=(c == 0), stop=(c == GB - 1))
                mm.then_inc(logits_ready, 1)
            pe.wait_ge(picked, 1)
            for g in range(G):
                for n, src in enumerate((token, weight)):
                    nc.tensor.transpose(turned[2 * g + n][:, 0:P], src[g][:].rearrange("p a s -> p (a s)"),
                                        ident[:]).then_inc(rows_turned, 1)

        @block.vector
        def _(dve):
            links = [0]

            def link(op):
                links[0] += 1
                op.then_inc(chain, 1)
                dve.wait_ge(chain, links[0])

            dve.wait_ge(logits_ready, G)
            for g in range(G):
                op = nc.vector.tensor_reduce(nmax[:, g:g + 1], logits[g][:, 0:S], AX.X, ALU.max)
            link(op)
            nc.vector.tensor_scalar(nmax[:], nmax[:], -1.0, None, ALU.mult).then_inc(nmax_ready, 1)
            dve.wait_ge(exp_done, G)
            link(nc.vector.reciprocal(total[:], total[:]))
            for g in range(G):
                op = nc.vector.tensor_scalar(p[g][:], p[g][:], total[:, g:g + 1], None, ALU.mult)
            link(op)
            for r in range(CAP // 8):
                cols = slice(8 * r, 8 * r + 8)
                for g in range(G):
                    op = nc.vector.max(top[g][:, cols], p[g][:])
                link(op)
                for g in range(G):
                    nc.vector.max_index(where[g][:, cols], top[g][:, cols], p[g][:])
                    op = nc.vector.match_replace(p[g][:], top[g][:, cols], p[g][:], -1.0)
                link(op)
            for g in range(G):
                for a in range(2):
                    nc.vector.tensor_copy(token[g][:, a, :], where[g][:])
                op = nc.vector.tensor_reduce(wsum[:, g:g + 1], top[g][:], AX.X, ALU.add)
            link(op)
            link(nc.vector.tensor_scalar(wsum[:], wsum[:], 1e-9, None, ALU.add))
            link(nc.vector.reciprocal(wsum[:], wsum[:]))
            for g in range(G):
                for a in range(2):
                    op = nc.vector.tensor_scalar(weight[g][:, a, :], top[g][:], wsum[:, g:g + 1], None, ALU.mult)
            op.then_inc(picked, 1)
            for g in range(G):
                cs = slice(g * GB // 2, (g + 1) * GB // 2)
                dve.wait_ge(rows_turned, 2 * g + 2)
                dve.wait_ge(rw2_in, 48)
                for a in range(2):
                    half = slice(CAP * a, CAP * a + CAP)
                    tok, wgt = (turned[2 * g + n][half, 0:P].rearrange("p (c a e) -> p e c a", a=2, e=NE)[:, :, :, a]
                                for n in range(2))
                    base = row_base[half, cs].unsqueeze(1).to_broadcast([CAP, NE, GB // 2])
                    nc.vector.tensor_tensor(row_of[half, :, cs], tok, base, ALU.add)
                    nc.vector.tensor_scalar(slot_of[half, :, cs], tok, slot_base[half, 0:1], None, ALU.add)
                    op = nc.vector.tensor_copy(weight_of[half, :, cs], wgt)
            link(op)


def experts(nc, dram, keep):
    CB = NC2 // 2
    W = CB * P
    with ExitStack() as ctx:
        def sb(name, *shape, dt=F32):
            return ctx.enter_context(nc.sbuf_tensor(name, [P, *shape], dt))

        def ps(name):
            return ctx.enter_context(nc.psum_tensor(name, [P, 512], F32))

        def sem(name):
            return ctx.enter_context(nc.semaphore(name))

        ident, row_of, slot_of, weight_of = keep["ident"], keep["row_of"], keep["slot_of"], keep["weight_of"]
        SHAPES = ((KT, FF), (KT, FF), (FT, D))
        raw = [sb(f"raw{n}", *shape) for n, shape in enumerate(SHAPES)]
        w_hi = [[sb(f"w_hi{e}{n}", *shape, dt=F32R) for n, shape in enumerate(SHAPES)] for e in range(2)]
        w_lo = [[sb(f"w_lo{e}{n}", *shape, dt=F32R) for n, shape in enumerate(SHAPES)] for e in range(2)]
        rows_now = [sb(f"rows_now{n}", NC2, dt=U32) for n in range(2)]
        slots_now = [sb(f"slots_now{n}", NC2, dt=U32) for n in range(2)]
        rows = sb("rows", NC2, D)
        xT_hi = [sb(f"xT_hi{n}", KT, W, dt=F32R) for n in range(2)]
        xT_lo = [sb(f"xT_lo{n}", KT, W, dt=F32R) for n in range(2)]
        gate = [sb(f"gate{n}", W) for n in range(2)]
        hidden = [sb(f"hidden{n}", W) for n in range(2)]
        h_hi = [sb(f"h_hi{n}", FT, W, dt=F32R) for n in range(2)]
        h_lo = [sb(f"h_lo{n}", FT, W, dt=F32R) for n in range(2)]
        y = [sb(f"y{m}", D) for m in range(CB)]
        last = sb("last", 2, CB * 2 * TT, D)
        NT = CB * 2 * TT
        stats, mv, rstd = sb("stats3", 2, NT, 6), sb("mv3", 2, NT, 2), sb("rstd3", 2, NT)
        log, guess, newton = sb("log3", 2, NT), sb("guess3", 2, NT), sb("newton3", 2, NT)
        gate_bank = [ps(f"gate_bank{n}") for n in range(2)]
        value_bank = [ps(f"value_bank{n}") for n in range(2)]
        turn_bank = [ps(f"turn_bank{n}") for n in range(KT)]
        y_bank = [ps(f"y_bank{n}") for n in range(2)]

        raw_in, w_hi_ready, w_lo_ready = sem("raw_in"), sem("w_hi_ready"), sem("w_lo_ready")
        rows_taken, slots_taken, pool_met = sem("rows_taken"), sem("slots_taken"), sem("pool_met3")
        rows_in = [sem(f"rows_in{n}") for n in range(2)]
        rows_turned, xT_hi_ready, xT_lo_ready = sem("rows_turned3"), sem("xT_hi_ready"), sem("xT_lo_ready")
        product_ready, gate_ready, hidden_ready = sem("product_ready"), sem("gate_ready"), sem("hidden_ready")
        h_hi_ready, h_lo_ready = sem("h_hi_ready"), sem("h_lo_ready")
        y_ready, y_scaled = sem("y_ready"), sem("y_scaled")
        added = [sem(f"added{c}") for c in range(NC2)]
        last_in = [sem(f"last_in{n}") for n in range(2)]
        log_chain, guess_ready, newton_chain = sem("log_chain3"), sem("guess_ready3"), sem("newton_chain3")
        ln, rstd_ready, ln_done, out_done = sem("ln"), sem("rstd_ready3"), sem("ln_done"), sem("out_done")

        block = ctx.enter_context(nc.Block())

        def all_experts(eng, expert):
            for e in range(2):
                expert(Iter(0, e))
            with eng.Fori(1, NE // 2 - 1) as j:
                for r in range(2):
                    expert(Iter(j, r))
            for e in range(NE - 2, NE):
                expert(Iter(0, e))

        @block.sync
        def _(sp):
            def load(it):
                if it.at_least(1):
                    sp.wait_ge(w_lo_ready, it.lin(3, 0))
                for n, name in enumerate(("w1", "w2", "w3")):
                    src = dram[name][bass.ds(it.i, 1)].rearrange("o (k p) f -> p (o k) f", p=P)
                    sp.dma_start(raw[n][:], src).then_inc(raw_in, 16)

            all_experts(sp, load)
            for h in range(2):
                for m in range(CB):
                    c = CB * h + m
                    sp.wait_ge(added[c], 16 * NE)
                    sp.dma_start(last[:, h, m * 2 * TT:(m + 1) * 2 * TT, :],
                                 dram["acc"][c].rearrange("(t p) d -> p t d", p=P)).then_inc(last_in[h], 16)
            for h in range(2):
                sp.wait_ge(ln_done, h + 1)
                sp.dma_start(dram["out"][h * NB // 2:(h + 1) * NB // 2].rearrange("b (t p) d -> p (b t) d", p=P),
                             last[:, h, :, :]).then_inc(out_done, 16)
            sp.wait_ge(out_done, 32)

        @block.gpsimd
        def _(pool):
            def gather(it, h):
                par = it.r % 2
                if it.at_least(1):
                    pool.wait_ge(rows_turned, it.lin(2 * KT, (h - 1) * KT))
                    pool.sem_inc(pool_met, 1)
                for m in range(CB):
                    c = CB * h + m
                    nc.gpsimd.indirect_dma_start(
                        rows[:, c, :], None, dram["x2"],
                        bass.IndirectOffsetOnAxis(ap=rows_now[par][:, c:c + 1], axis=0)).then_inc(rows_in[h], 16)

            def take(it, now, source, taken):
                now = now[it.r % 2]
                nc.gpsimd.tensor_copy(now[:], source[:, bass.ds(it.i, 1), :].rearrange("p o c -> p (o c)")).then_inc(taken, 1)
                pool.wait_ge(taken, it.lin(1, 1))
                pool.sem_inc(pool_met, 1)

            def scatter(it, h):
                for m in range(CB):
                    c = CB * h + m
                    if it.at_least(1):
                        pool.wait_ge(added[c], it.lin(16, 0))
                    pool.wait_ge(y_scaled, it.lin(2 * CB, CB * h + m + 1))
                    pool.sem_inc(pool_met, 1)
                    nc.gpsimd.indirect_dma_start(
                        dram["acc"][c], bass.IndirectOffsetOnAxis(ap=slots_now[it.r % 2][:, c:c + 1], axis=0),
                        y[m][:], None, compute_op=ALU.add).then_inc(added[c], 16)

            def expert(it):
                more = not it.fixed or it.i < NE - 1
                nxt = Iter(it.j, it.r + 1)
                if more:
                    if it.at_least(1):
                        pool.wait_ge(rows_turned, it.lin(2 * KT, 0))
                    take(nxt, rows_now, row_of, rows_taken)
                    gather(nxt, 0)
                if it.at_least(1):
                    scatter(Iter(it.j, it.r - 1), 1)
                if more:
                    gather(nxt, 1)
                take(it, slots_now, slot_of, slots_taken)
                scatter(it, 0)

            take(Iter(0, 0), rows_now, row_of, rows_taken)
            for h in range(2):
                gather(Iter(0, 0), h)
            all_experts(pool, expert)
            scatter(Iter(0, NE - 1), 1)
            for h in range(2):
                pool.wait_ge(guess_ready, h + 1)
                refine_deviation(pool, lambda: None, mv[:, h, :, 1], guess[:, h, :], newton[:, h, :], rstd[:, h, :],
                                 newton_chain, 3 * h, rstd_ready)

        @block.tensor
        def _(pe):
            def product(out, pairs):
                n = 0
                for a, b in pairs:
                    for x, z in ((0, 0), (0, 1), (1, 0)):
                        n += 1
                        mm = nc.tensor.matmul(out, a[x], b[z], start=(n == 1), stop=(n == 3 * len(pairs)))
                return mm

            def turn(it, h):
                pe.wait_ge(rows_in[h], it.lin(16 * CB, 16 * CB))
                for k in range(KT):
                    if it.at_least(1) or h:
                        pe.wait_ge(xT_lo_ready, it.lin(2 * KT, (h - 1) * KT + k + 1))
                    for m in range(CB):
                        mm = nc.tensor.transpose(turn_bank[k][:, m * P:(m + 1) * P],
                                                 rows[:, CB * h + m, k * P:(k + 1) * P], ident[:])
                    mm.then_inc(rows_turned, 1)

            def up(it, h):
                par = it.r % 2
                pe.wait_ge(xT_lo_ready, it.lin(2 * KT, (h + 1) * KT))
                if h == 0:
                    pe.wait_ge(w_lo_ready, it.lin(3, 2))
                for f in range(FT):
                    if it.at_least(1) or h or f >= 2:
                        pe.wait_ge(gate_ready, it.lin(2 * FT, FT * h + f - 1))
                        pe.wait_ge(hidden_ready, it.lin(2 * FT, FT * h + f - 1))
                    cols = slice(f * P, (f + 1) * P)
                    for n, out in ((0, gate_bank[f % 2]), (1, value_bank[f % 2])):
                        mm = product(out[:], [((w_hi[par][n][:, k, cols], w_lo[par][n][:, k, cols]),
                                               (xT_hi[h][:, k, :], xT_lo[h][:, k, :])) for k in range(KT)])
                    mm.then_inc(product_ready, 1)

            def down(it, h):
                par = it.r % 2
                if h == 0:
                    pe.wait_ge(w_lo_ready, it.lin(3, 3))
                pe.wait_ge(h_lo_ready, it.lin(2 * FT, FT * (h + 1)))
                for m in range(CB):
                    if it.at_least(1) or h or m >= 2:
                        pe.wait_ge(y_scaled, it.lin(2 * CB, CB * h + m - 1))
                    cols = slice(m * P, (m + 1) * P)
                    mm = product(y_bank[m % 2][:, 0:D], [((h_hi[h][:, f, cols], h_lo[h][:, f, cols]),
                                                          (w_hi[par][2][:, f, :], w_lo[par][2][:, f, :])) for f in range(FT)])
                    mm.then_inc(y_ready, 1)

            def expert(it):
                up(it, 0)
                turn(it, 1)
                if it.at_least(1):
                    down(Iter(it.j, it.r - 1), 1)
                up(it, 1)
                if not it.fixed or it.i < NE - 1:
                    turn(Iter(it.j, it.r + 1), 0)
                down(it, 0)

            turn(Iter(0, 0), 0)
            all_experts(pe, expert)
            down(Iter(0, NE - 1), 1)

        @block.scalar
        def _(act):
            def split_weights(it):
                par = it.r % 2
                act.wait_ge(raw_in, it.lin(48, 48))
                if it.at_least(2):
                    act.wait_ge(y_ready, it.lin(2 * CB, -2 * CB))
                for n in range(3):
                    nc.scalar.copy(w_hi[par][n][:], raw[n][:]).then_inc(w_hi_ready, 1)

            def columns(it, h):
                if it.at_least(1):
                    act.wait_ge(product_ready, it.lin(2 * FT, FT * (h - 1)))
                for k in range(KT):
                    act.wait_ge(rows_turned, it.lin(2 * KT, h * KT + k + 1))
                    nc.scalar.copy(xT_hi[h][:, k, :], turn_bank[k][:]).then_inc(xT_hi_ready, 1)

            def h_high(it, h, f):
                act.wait_ge(hidden_ready, it.lin(2 * FT, FT * h + f + 1))
                if f == 0 and it.at_least(1):
                    act.wait_ge(y_ready, it.lin(2 * CB, CB * (h - 1)))
                nc.scalar.copy(h_hi[h][:, f, :], hidden[f % 2][:]).then_inc(h_hi_ready, 1)

            def weigh(it, h):
                for m in range(CB):
                    act.wait_ge(y_ready, it.lin(2 * CB, CB * h + m + 1))
                    if h:
                        act.wait_ge(added[m], it.lin(16, 16))
                    elif it.at_least(1):
                        act.wait_ge(added[CB + m], it.lin(16, 0))
                    nc.scalar.activation(y[m][:], y_bank[m % 2][:, 0:D], ACT.Copy,
                                         scale=weight_of[:, bass.ds(it.i, 1), CB * h + m]).then_inc(y_scaled, 1)

            def gates(it, h):
                for f in range(FT):
                    act.wait_ge(product_ready, it.lin(2 * FT, FT * h + f + 1))
                    if it.at_least(1) or h or f >= 2:
                        act.wait_ge(hidden_ready, it.lin(2 * FT, FT * h + f - 1))
                    nc.scalar.activation(gate[f % 2][:], gate_bank[f % 2][:], ACT.Silu).then_inc(gate_ready, 1)
                    if f:
                        h_high(it, h, f - 1)
                h_high(it, h, FT - 1)

            def expert(it):
                gates(it, 0)
                columns(it, 1)
                if it.at_least(1):
                    weigh(Iter(it.j, it.r - 1), 1)
                more = not it.fixed or it.i < NE - 1
                if more:
                    split_weights(Iter(it.j, it.r + 1))
                gates(it, 1)
                if more:
                    columns(Iter(it.j, it.r + 1), 0)
                weigh(it, 0)

            split_weights(Iter(0, 0))
            columns(Iter(0, 0), 0)
            act.preload_act_table(ACT.Silu)
            all_experts(act, expert)
            weigh(Iter(0, NE - 1), 1)
            act.preload_act_table_set("natural_log_exp_and_others")
            for h in range(2):
                act.wait_ge(ln, 2 * h + 2)
                estimate_deviation(act, mv[:, h, :, 1], log[:, h, :], guess[:, h, :], log_chain, h, guess_ready)

        @block.vector
        def _(dve):
            def split_weights(it):
                par = it.r % 2
                for n in range(3):
                    dve.wait_ge(w_hi_ready, it.lin(3, n + 1))
                    nc.vector.tensor_tensor(w_lo[par][n][:], raw[n][:], w_hi[par][n][:], ALU.subtract).then_inc(w_lo_ready, 1)

            def columns(it, h):
                for k in range(KT):
                    dve.wait_ge(xT_hi_ready, it.lin(2 * KT, h * KT + k + 1))
                    nc.vector.tensor_tensor(xT_lo[h][:, k, :], turn_bank[k][:], xT_hi[h][:, k, :],
                                            ALU.subtract).then_inc(xT_lo_ready, 1)

            def h_low(it, h, f):
                dve.wait_ge(h_hi_ready, it.lin(2 * FT, FT * h + f + 1))
                nc.vector.tensor_tensor(h_lo[h][:, f, :], hidden[f % 2][:], h_hi[h][:, f, :],
                                        ALU.subtract).then_inc(h_lo_ready, 1)

            def multiply(it, h):
                for f in range(FT):
                    dve.wait_ge(gate_ready, it.lin(2 * FT, FT * h + f + 1))
                    if it.at_least(1) or h or f >= 2:
                        dve.wait_ge(h_lo_ready, it.lin(2 * FT, FT * h + f - 1))
                    nc.vector.tensor_tensor(hidden[f % 2][:], gate[f % 2][:], value_bank[f % 2][:],
                                            ALU.mult).then_inc(hidden_ready, 1)
                    if f:
                        h_low(it, h, f - 1)
                h_low(it, h, FT - 1)

            def expert(it):
                multiply(it, 0)
                columns(it, 1)
                more = not it.fixed or it.i < NE - 1
                if more:
                    split_weights(Iter(it.j, it.r + 1))
                multiply(it, 1)
                if more:
                    columns(Iter(it.j, it.r + 1), 0)

            split_weights(Iter(0, 0))
            columns(Iter(0, 0), 0)
            all_experts(dve, expert)

            for h in range(2):
                dve.wait_ge(last_in[h], 16 * CB)
                for t in range(NT):
                    op = nc.vector.bn_stats(stats[:, h, t, :], last[:, h, t, :])
                op.then_inc(ln, 1)
                dve.wait_ge(ln, 2 * h + 1)
                for t in range(NT):
                    op = nc.vector.bn_aggr(mv[:, h, t, :], stats[:, h, t, :])
                op.then_inc(ln, 1)
            for h in range(2):
                dve.wait_ge(rstd_ready, h + 1)
                for t in range(NT):
                    op = nc.vector.tensor_scalar(last[:, h, t, :], last[:, h, t, :], mv[:, h, t, 0:1],
                                                 rstd[:, h, t:t + 1], ALU.subtract, ALU.mult)
                op.then_inc(ln_done, 1)


def program(nc, dram):
    with ExitStack() as ctx:
        def sb(name, *shape):
            return ctx.enter_context(nc.sbuf_tensor(name, [P, *shape], F32))

        keep = {"ident": sb("ident", P)}
        with nc.sbuf_tensor("r1", [P, NB * S], F32) as r1:
            keep["r1"] = r1
            mixing(nc, dram, keep)
            with ExitStack() as later:
                for name, dt in (("row_of", U32), ("slot_of", U32), ("weight_of", F32)):
                    keep[name] = later.enter_context(nc.sbuf_tensor(name, [P, NE, NC2], dt))
                routing(nc, dram, keep)
                experts(nc, dram, keep)


def kernel(**inputs):
    import numpy as np
    import concourse.bacc as bacc
    from concourse.bass_utils import run_bass_kernel_spmd

    a = {k: np.asarray(v) for k, v in inputs.items()}
    c = np.ascontiguousarray

    def by_parity(w):
        order = [4 * k + 2 * f + a for f in range(KT) for a in range(2) for k in range(HG)]
        return w.reshape(*w.shape[:-1], NH, DH)[..., order, :].reshape(w.shape)

    arrays = {
        "x": c(a["x"]), "xT": c(a["x"].transpose(0, 2, 1)), "cT": c(a["ctx_1024"].transpose(0, 2, 1)),
        "mix_A": c(a["L0_attn_A"].reshape(KT, P).T), "mix_BT": c(a["L0_attn_B"].T), "mix_WT": c(a["L0_attn_W"].T), "mix_b": c(a["L0_attn_b"]),
        "WqT": c(by_parity(a["L0_xattn_Wq"].T)), "bq": c(by_parity(a["L0_xattn_bq"]).reshape(KT, P).T), "WkT": c(by_parity(a["L0_xattn_Wk"].T)), "bk": c(by_parity(a["L0_xattn_bk"]).reshape(KT, P).T),
        "WvT": c(a["L0_xattn_Wv"].T), "bv": c(a["L0_xattn_bv"]), "WoT": c(a["L0_xattn_Wo"].T), "bo": c(a["L0_xattn_bo"]),
        "rw1": c(a["L0_ffn_router_w1"]), "rw2": c(a["L0_ffn_router_w2"]),
        "w1": c(a["L0_ffn_w1"]), "w2": c(a["L0_ffn_w2"]), "w3": c(a["L0_ffn_w3"]),
    }
    rows = np.arange(P)
    freq = (np.float32(1.0) / np.power(np.float32(10000.0), np.arange(0, DH, 2, dtype=np.float32) / np.float32(DH))).astype(np.float32)
    angle = (freq[rows % (DH // 2)][:, None] * np.arange(S, dtype=np.float32)[None, :]).astype(np.float32)
    sign = np.where(rows % DH < DH // 2, -1.0, 1.0)[:, None]
    pos = np.arange(S)
    arrays["cos"] = np.cos(angle.astype(np.float64)).astype(np.float32)
    arrays["sin"] = (sign * np.sin(angle.astype(np.float64))).astype(np.float32)
    keys = (pos[:, None] // P) * FIRST + np.arange(SPAN)[None, :]
    arrays["band"] = np.where(np.abs(pos[:, None] - keys) <= WINDOW, 0.0, MASKED).astype(np.float32)
    arrays["ident"] = np.eye(P, dtype=np.float32)
    arrays["slot_base"] = (S * (rows[:, None] // CAP)).astype(np.float32)
    arrays["row_base"] = (arrays["slot_base"] + 2 * S * np.arange(NC2)[None, :]).astype(np.float32)

    nc = bacc.Bacc("TRN2", target_bir_lowering=False, num_devices=1)
    dram = {k: nc.dram_tensor(f"in_{k}", v.shape, F32, kind="ExternalInput").ap() for k, v in arrays.items()}
    dram["parts"] = nc.dram_tensor("rotated_parts", (2, 2, P, KT * S), F32, kind="Internal").ap()
    dram["x2"] = nc.dram_tensor("x2_rows", (NB * S, D), F32, kind="Internal").ap()
    dram["acc"] = [nc.dram_tensor(f"acc_rows{c}", (2 * S, D), F32, kind="Internal").ap() for c in range(NC2)]
    dram["out"] = nc.dram_tensor("out_0", (NB, S, D), F32, kind="ExternalOutput").ap()
    program(nc, dram)
    r = run_bass_kernel_spmd(nc, [{f"in_{k}": v for k, v in arrays.items()}], core_ids=[0])
    return r.results[0]["out_0"]
```
